# Optimizing a Trainium2 kernel written in Bass

```python
import numpy as np
import jax
import jax.numpy as jnp

def _softmax(x, axis=-1):
    return jax.nn.softmax(x, axis=axis)

def _gelu(x):
    return jax.nn.gelu(x, approximate=True)

def _silu(x):
    return jax.nn.silu(x)

def _sigmoid(x):
    return jax.nn.sigmoid(x)

def _layernorm(x, axis=-1, eps=1e-05):
    m = jnp.mean(x, axis=axis, keepdims=True)
    v = jnp.var(x, axis=axis, keepdims=True)
    return (x - m) / jnp.sqrt(v + eps)

def _scatter_add(tgt, idx, src, axis=0):
    return tgt.at[idx].add(src)

def _segment_sum(src, seg, n):
    return jax.ops.segment_sum(src, seg, n)
kernel_name = 'mk_xattn_seq_d1_seqx_r4_00811d'

def setup_inputs(seed: int=0):
    np.random.seed(seed)
    _w = jnp.asarray

    def _rec_inputs():
        import jax
        import jax.numpy as jnp
        _rk = jax.random.key(seed)
        x = 7.22e-05 + 1 * jax.random.normal(jax.random.fold_in(_rk, 1), (4, 512, 256), jnp.float32)
        _lenS = 512 - jax.random.randint(jax.random.fold_in(_rk, 7), (4,), 0, max(1, 512 // 4) + 1, jnp.int32)
        _lenS2 = 512 - jax.random.randint(jax.random.fold_in(_rk, 8), (4,), 0, max(1, 512 // 4) + 1, jnp.int32)
        _ctx_1024P = jax.random.normal(jax.random.fold_in(_rk, 11), (4, 16, 256), jnp.float32)
        _ctx_1024c = jax.random.dirichlet(jax.random.fold_in(_rk, 511), 0.3 * jnp.ones((16,), jnp.float32), (4, 512))
        _ctx_1024t = jnp.einsum('bsk,bkd->bsd', _ctx_1024c, _ctx_1024P)
        _ctx_1024t = _ctx_1024t * jax.lax.rsqrt(jnp.mean(jnp.square(_ctx_1024t)) + 1e-12) * 0.953939
        ctx_1024 = 4.13588e-05 + 0.999923 * (_ctx_1024t + 0.3 * jax.random.normal(jax.random.fold_in(_rk, 611), (4, 512, 256), jnp.float32))
        return (x, ctx_1024)
    x, ctx_1024 = _rec_inputs()

    def _L0_xattn_setup():
        import jax, jax.numpy as jnp
        import numpy as np
        H_S = 256
        N_HEADS = 16
        P_S = H_S // N_HEADS
        LN_EPS = 1e-05

        def layer_norm(x, gamma, beta):
            mu = jnp.mean(x, axis=-1, keepdims=True)
            var = jnp.var(x, axis=-1, keepdims=True)
            return (x - mu) * jax.lax.rsqrt(var + LN_EPS) * gamma + beta

        def _split_heads(x):
            b, s, _ = x.shape
            return x.reshape(b, s, N_HEADS, P_S).transpose(0, 2, 1, 3)
        key = jax.random.key(seed)
        ks = jax.random.split(key, 8)
        scale = 1.0 / np.sqrt(H_S)
        B, S = (4, 512)
        return {'q': jax.random.normal(ks[0], (B, S, H_S), jnp.float32), 'k': jax.random.normal(ks[1], (B, S, H_S), jnp.float32), 'v': jax.random.normal(ks[2], (B, S, H_S), jnp.float32), 'ln_q_g': jnp.ones((H_S,), jnp.float32), 'ln_q_b': jnp.zeros((H_S,), jnp.float32), 'ln_k_g': jnp.ones((H_S,), jnp.float32), 'ln_k_b': jnp.zeros((H_S,), jnp.float32), 'ln_v_g': jnp.ones((H_S,), jnp.float32), 'ln_v_b': jnp.zeros((H_S,), jnp.float32), 'w_q': jax.random.normal(ks[3], (H_S, H_S), jnp.float32) * scale, 'w_k': jax.random.normal(ks[4], (H_S, H_S), jnp.float32) * scale, 'w_v': jax.random.normal(ks[5], (H_S, H_S), jnp.float32) * scale, 'w_fc': jax.random.normal(ks[6], (H_S, H_S), jnp.float32) * scale, 'b_fc': jnp.zeros((H_S,), jnp.float32)}
    _L0_xattn_all = _L0_xattn_setup()
    _L0_xattn_in = {k: v for k, v in _L0_xattn_all.items() if k in ('ln_q_g', 'ln_q_b', 'ln_k_g', 'ln_k_b', 'ln_v_g', 'ln_v_b', 'w_q', 'w_k', 'w_v', 'w_fc', 'b_fc')}
    del _L0_xattn_all
    return {'x': x, 'ctx_1024': ctx_1024, 'L0_xattn_ln_q_g': _L0_xattn_in['ln_q_g'], 'L0_xattn_ln_q_b': _L0_xattn_in['ln_q_b'], 'L0_xattn_ln_k_g': _L0_xattn_in['ln_k_g'], 'L0_xattn_ln_k_b': _L0_xattn_in['ln_k_b'], 'L0_xattn_ln_v_g': _L0_xattn_in['ln_v_g'], 'L0_xattn_ln_v_b': _L0_xattn_in['ln_v_b'], 'L0_xattn_w_q': _L0_xattn_in['w_q'], 'L0_xattn_w_k': _L0_xattn_in['w_k'], 'L0_xattn_w_v': _L0_xattn_in['w_v'], 'L0_xattn_w_fc': _L0_xattn_in['w_fc'], 'L0_xattn_b_fc': _L0_xattn_in['b_fc']}

def reference(x, ctx_1024, L0_xattn_ln_q_g, L0_xattn_ln_q_b, L0_xattn_ln_k_g, L0_xattn_ln_k_b, L0_xattn_ln_v_g, L0_xattn_ln_v_b, L0_xattn_w_q, L0_xattn_w_k, L0_xattn_w_v, L0_xattn_w_fc, L0_xattn_b_fc):
    import jax
    import jax.numpy as jnp

    def _L0_xattn_ref(q, k, v, ln_q_g, ln_q_b, ln_k_g, ln_k_b, ln_v_g, ln_v_b, w_q, w_k, w_v, w_fc, b_fc):
        import jax, jax.numpy as jnp
        import numpy as np
        H_S = 256
        N_HEADS = 16
        P_S = H_S // N_HEADS
        LN_EPS = 1e-05

        def layer_norm(x, gamma, beta):
            mu = jnp.mean(x, axis=-1, keepdims=True)
            var = jnp.var(x, axis=-1, keepdims=True)
            return (x - mu) * jax.lax.rsqrt(var + LN_EPS) * gamma + beta

        def _split_heads(x):
            b, s, _ = x.shape
            return x.reshape(b, s, N_HEADS, P_S).transpose(0, 2, 1, 3)
        b, q_l, _ = q.shape
        qh = _split_heads(layer_norm(q, ln_q_g, ln_q_b) @ w_q.T)
        kh = _split_heads(layer_norm(k, ln_k_g, ln_k_b) @ w_k.T)
        vh = _split_heads(layer_norm(v, ln_v_g, ln_v_b) @ w_v.T)
        scores = jnp.einsum('bhqp,bhkp->bhqk', qh, kh) / jnp.sqrt(jnp.float32(P_S))
        attn = jax.nn.softmax(scores, axis=-1)
        ctx = jnp.einsum('bhqk,bhkp->bhqp', attn, vh)
        ctx = ctx.transpose(0, 2, 1, 3).reshape(b, q_l, H_S)
        out = ctx @ w_fc.T + b_fc
        return q + out
    x = _L0_xattn_ref(x, ctx_1024, ctx_1024, L0_xattn_ln_q_g, L0_xattn_ln_q_b, L0_xattn_ln_k_g, L0_xattn_ln_k_b, L0_xattn_ln_v_g, L0_xattn_ln_v_b, L0_xattn_w_q, L0_xattn_w_k, L0_xattn_w_v, L0_xattn_w_fc, L0_xattn_b_fc)
    return x

_drawn_inputs = setup_inputs


def setup_inputs(seed=0):
    import zlib

    import numpy as np

    out = dict(_drawn_inputs(seed))
    spreads = {'L0_xattn_ln_q_g': (1.0, 0.2),
     'L0_xattn_ln_q_b': (0.0, 0.525),
     'L0_xattn_ln_k_g': (1.0, 0.2),
     'L0_xattn_ln_k_b': (0.0, 0.8),
     'L0_xattn_ln_v_g': (1.0, 0.2),
     'L0_xattn_ln_v_b': (0.0, 0.1),
     'L0_xattn_b_fc': (0.0, 0.1)}
    factors = {}
    for name, (base, spread) in spreads.items():
        noise = np.random.default_rng([zlib.crc32(name.encode()), seed]).standard_normal(out[name].shape)
        drawn = base * np.exp(spread * noise) if base else spread * noise
        out[name] = jnp.asarray(drawn.astype(out[name].dtype))
    for name, factor in factors.items():
        out[name] = (out[name] * factor).astype(out[name].dtype)
    return out
```

```python
from contextlib import ExitStack

import concourse.bass as bass
from concourse import mybir

F32 = mybir.dt.float32
BF16 = mybir.dt.bfloat16
ALU = mybir.AluOpType
ACT = mybir.ActivationFunctionType
AX = mybir.AxisListType

P = 128
B, S, DM = 4, 512, 256
HEADS, HD = 16, 16
G = 4
UNITS = HEADS // G
T = S // P
FT = DM // P
ROWS = 6 * HD
MROWS = 3
TILES = T * G
LEAD = 28
EPS = 1e-5
SCALE = float(HD) ** -0.5
QPARTS = ((0, 0, 3), (3, 1, 2), (5, 2, 1))
DMA = 16


def build(nc, x, ctx_in, wq, wk, wv, wfc, ln_cols, b_fc, eye, out):
    with ExitStack() as stack:
        def sb(name, shape, dt=F32):
            return stack.enter_context(nc.sbuf_tensor(name, shape, dt))

        def sem(name):
            return stack.enter_context(nc.semaphore(name))

        q_rows = nc.dram_tensor("q_rows", (B, 2, 6, HD, HEADS // 2, S), BF16, kind="Internal").ap()
        k_rows = nc.dram_tensor("k_rows", (B, 2, 6, HD, HEADS // 2, S), BF16, kind="Internal").ap()
        unit_out = nc.dram_tensor("unit_out", (B, UNITS, G, 32, S), F32, kind="Internal").ap()
        recip_rows = nc.dram_tensor("recip_rows", (B, HEADS, S), F32, kind="Internal").ap()

        ident = sb("ident", [P, P])
        ident_b = sb("ident_b", [P, P], BF16)
        w_sb = {n: sb("w_" + n, [P, FT, DM]) for n in ("q", "k", "v", "fc")}
        lnc = sb("lnc", [P, 6, FT])
        bias = sb("bias", [P, DM])
        eps = sb("eps", [P, 1])
        warm = sb("warm", [P, 1])
        xin = sb("xin", [P, B * T, DM])
        cin = sb("cin", [P, B * T, DM])
        xn = sb("xn", [P, 2, T, DM])
        stats = sb("stats", [P, 2 * T, 6])
        mv = sb("mv", [P, 2 * T, 2])
        std = sb("std", [P, 2 * T])
        newton = sb("newton", [P, 4, 2 * T])
        rstd = sb("rstd", [P, 2 * T])
        lnT = sb("lnT", [P, 3, FT, S])
        parts = sb("parts", [P, 4, 3, S], BF16)
        rest = sb("rest", [P, 2, S])
        v_all = sb("v_all", [P, B * T, DM])
        qs = sb("qs", [P, UNITS, G, S], BF16)
        ks = sb("ks", [P, UNITS, G, S], BF16)
        neg_max = sb("neg_max", [P, 4, G, T])
        m_rest = sb("m_rest", [P, 2, G * T])
        m_parts = sb("m_parts", [P, 2, MROWS, G * T], BF16)
        m_rows = sb("m_rows", [MROWS * G * T, 2, P], BF16)
        v_st = sb("v_st", [P, UNITS, T, G, 32])
        zeros = sb("zeros", [P, T * G * HD])
        probs = sb("probs", [P, 4, G, S])
        o_sb = sb("o_sb", [P, 2, S])
        heads_out = cin[:, :, :].rearrange("p a b -> p (a b)").rearrange("p (h t) -> p h t", h=2)
        sums = sb("sums", [P, B, S // 8])
        recips = sb("recips", [P, B, S // 8])
        r_all = sb("r_all", [P, 2, B * S])
        ctxT = sb("ctxT", [P, 2, 2, S])

        ps = stack.enter_context(nc.psum_tensor("ps", [P, 8, S], F32))
        trn, trn_last = [ps[:, k] for k in (0, 1, 2, 3)], [ps[:, k] for k in (0, 1, 6, 7)]
        prj, prj_last = [ps[:, k] for k in (4, 5, 4, 5)], [ps[:, k] for k in (0, 1, 6, 7)]
        vps, vps_last = [ps[:, k] for k in (6, 7)], [ps[:, k] for k in (0, 1)]
        st_ps = [ps[:, k] for k in range(2)]
        mx_ps = [ps[:, 2 + 2 * k:4 + 2 * k] for k in range(2)]
        pv_ps = ps[:, 6]
        mt_ps = ps[:, 7, 0:P // 2].bitcast(BF16)

        s_lx, s_lc, s_cst, s_w = sem("s_lx"), sem("s_lc"), sem("s_cst"), sem("s_w")
        s_ib, s_eps = sem("s_ib"), sem("s_eps")
        s_bs, s_mv, s_sd, s_nw, s_xn = sem("s_bs"), sem("s_mv"), sem("s_sd"), sem("s_nw"), sem("s_xn")
        s_tr, s_tev, s_prj, s_vprj, s_vev = sem("s_tr"), sem("s_tev"), sem("s_prj"), sem("s_vprj"), sem("s_vev")
        s_p1, s_rest, s_p2, s_p3, s_xr = sem("s_p1"), sem("s_rest"), sem("s_p2"), sem("s_p3"), sem("s_xr")
        s_pw = [sem(f"s_pw{k}") for k in range(4)]
        s_load = [sem(f"s_load{g}") for g in range(UNITS)]
        s_mrow = [sem(f"s_mrow{g}") for g in range(UNITS)]
        s_ones, s_vones = sem("s_ones"), sem("s_vones")
        s_mx, s_red, s_mstep, s_mp, s_mt, s_mtev = (sem("s_mx"), sem("s_red"), sem("s_mstep"), sem("s_mp"),
                                                    sem("s_mt"), sem("s_mtev"))
        s_st, s_exp, s_vst, s_pv, s_oev = sem("s_st"), sem("s_exp"), sem("s_vst"), sem("s_pv"), sem("s_oev")
        s_ow = [sem(f"s_ow{k}") for k in range(2)]
        s_ds, s_rc, s_rw, s_rr = sem("s_ds"), sem("s_rc"), sem("s_rw"), sem("s_rr")
        s_ct, s_fc, s_fin, s_out = sem("s_ct"), sem("s_fc"), sem("s_fin"), sem("s_out")

        x_t = x.rearrange("b (t p) d -> b p t d", p=P)
        c_t = ctx_in.rearrange("b (t p) d -> b p t d", p=P)
        out_t = out.rearrange("b (t p) d -> b p t d", p=P)

        s_zero, s_warm = sem("s_zero"), sem("s_warm")
        s_own = {e: sem("s_own_" + e) for e in ("sp", "dve", "pe")}

        def wait_alone(eng, name, semaphore, value):
            eng.wait_ge(semaphore, value)
            eng.sem_inc(s_own[name], 1)

        block = stack.enter_context(nc.Block())

        @block.sync
        def _(sp):
            def load_inputs(b):
                sp.dma_start(xin[:, bass.ts(b, T)], x_t[b]).then_inc(s_lx, DMA)
                sp.dma_start(cin[:, bass.ts(b, T)], c_t[b]).then_inc(s_lc, DMA)

            def write_parts(b):
                for k in range(4):
                    wait_alone(sp, "sp", s_p3, 4 * b + k + 1)
                    if k < 2:
                        for row, part, n in QPARTS:
                            dst = q_rows[b, k % 2, row:row + n].rearrange("c d h t -> (d h) c t")
                            src = parts[:, k, part, :].unsqueeze(1).to_broadcast([P, n, S])
                            sp.dma_start(dst, src).then_inc(s_pw[k], DMA)
                    else:
                        for row, n in ((0, 3), (3, 2), (5, 1)):
                            dst = k_rows[b, k % 2, row:row + n].rearrange("c d h t -> (d h) c t")
                            sp.dma_start(dst, parts[:, k, 0:n, :]).then_inc(s_pw[k], DMA)

            def load_stacks(b, g):
                wait_alone(sp, "sp", s_pw[g // 2], 3 * DMA * (b + 1))
                wait_alone(sp, "sp", s_pw[2 + g // 2], 3 * DMA * (b + 1))
                for rows, dst in ((q_rows, qs), (k_rows, ks)):
                    sp.dma_start(dst[0:ROWS, g], rows[b, g // 2, :, :, bass.ts(g % 2, G)].rearrange("c d h t -> (c d) h t"))\
                      .then_inc(s_load[g], DMA)

            def write_max_rows(w, slot, par):
                wait_alone(sp, "sp", s_mtev, w + 1)
                sp.dma_start(qs[ROWS:ROWS + MROWS, slot], m_rows[:, par, :]).then_inc(s_mrow[slot], DMA)

            def store_unit(b, g):
                u = UNITS * b + g
                wait_alone(sp, "sp", s_oev, u + 1)
                sp.dma_start(unit_out[b, g].rearrange("j r t -> (j r) t"), o_sb[:, g % 2, :])\
                  .then_inc(s_ow[g % 2], DMA)
                wait_alone(sp, "sp", s_ow[g % 2], DMA * (2 * b + g // 2 + 1))
                wait_alone(sp, "sp", s_ds, 2 * DMA * u)
                rows = 64 * (g % 2)
                sp.dma_start(heads_out[rows:rows + 64, g // 2, bass.ts(b, S)], unit_out[b, g, :, 0:HD, :])\
                  .then_inc(s_ds, DMA)
                sp.dma_start(sums[32 * g:32 * g + 32, b, :],
                             unit_out[b, g, :, HD, :].rearrange("j (c w) -> j c w", c=8)).then_inc(s_ds, DMA)

            def spread_recips(b):
                wait_alone(sp, "sp", s_rc, b + 1)
                sp.dma_start(recip_rows[b].rearrange("h (c w) -> (h c) w", c=8), recips[:, b, :])\
                  .then_inc(s_rw, DMA)
                wait_alone(sp, "sp", s_rw, DMA * (b + 1))
                wait_alone(sp, "sp", s_rr, 2 * DMA * b)
                for half in range(2):
                    src = recip_rows[b, bass.ts(half, HEADS // 2), :].unsqueeze(1)\
                        .to_broadcast([HEADS // 2, HD, S])
                    sp.dma_start(r_all[:, half, bass.ts(b, S)], src).then_inc(s_rr, DMA)

            def batch(b, first=False, last=False):
                for g in range(UNITS):
                    if g and not last:
                        wait_alone(sp, "sp", s_st, TILES * (UNITS * b + g))
                        load_stacks(b + 1, g - 1)
                    if g:
                        store_unit(b, g - 1)
                    if not (last and g == UNITS - 1):
                        write_max_rows(UNITS * b + g + 1, (g + 1) % UNITS, (g + 1) % 2)
                if not first:
                    spread_recips(b - 1)
                if not last:
                    wait_alone(sp, "sp", s_st, TILES * UNITS * (b + 1))
                    load_stacks(b + 1, UNITS - 1)
                store_unit(b, UNITS - 1)

            load_inputs(0)
            sp.dma_start(ident[:, :], eye).then_inc(s_cst, DMA)
            sp.dma_start(lnc[:, :, :], ln_cols).then_inc(s_cst, DMA)
            for n, w in (("q", wq), ("k", wk), ("v", wv), ("fc", wfc)):
                sp.dma_start(w_sb[n][:, :, :], w.rearrange("(f p) n -> p f n", p=P)).then_inc(s_w, DMA)
            sp.dma_start(bias[:, :], b_fc.partition_broadcast(P)).then_inc(s_w, DMA)
            with sp.Fori(1, B) as i:
                wait_alone(sp, "sp", s_lx, DMA * i)
                wait_alone(sp, "sp", s_lc, DMA * i)
                load_inputs(i)
            with sp.Fori(0, 2) as i:
                write_parts(i)
            for g in range(UNITS):
                load_stacks(0, g)
            with sp.Fori(2, B) as i:
                write_parts(i)
            write_max_rows(0, 0, 0)
            batch(0, first=True)
            with sp.Fori(1, B - 1) as b:
                batch(b)
            batch(B - 1, last=True)
            spread_recips(B - 1)
            with sp.Fori(0, B) as b:
                for h in range(2):
                    wait_alone(sp, "sp", s_fin, 2 * b + h + 1)
                    sp.dma_start(out_t[b][:, bass.ts(h, 2)], xin[:, bass.ds(b * T + 2 * h, 2)])\
                      .then_inc(s_out, DMA)
            wait_alone(sp, "sp", s_out, DMA * 2 * B)

        @block.gpsimd
        def _(pool):
            nc.gpsimd.memset(ks[ROWS:P, :, :, :], 1.0).then_inc(s_ones, 1)
            pool.wait_ge(s_ones, 1)
            nc.gpsimd.memset(v_st[:, :, :, :, HD:32], 1.0).then_inc(s_vones, 1)
            nc.gpsimd.memset(zeros[:, :], 0.0).then_inc(s_zero, 1)
            pool.wait_ge(s_zero, 1)
            pool.wait_ge(s_w, 5 * DMA)
            with pool.Fori(0, B) as i:
                pool.wait_ge(s_xn, 2 * i + 1)
                nc.gpsimd.tensor_tensor(xin[:, bass.ts(i, T)], xin[:, bass.ts(i, T)],
                                        bias[:, :].unsqueeze(1).to_broadcast([P, T, DM]), ALU.add)\
                  .then_inc(s_xr, 1)
                for k in range(4):
                    pool.wait_ge(s_p2, 4 * i + k + 1)
                    nc.gpsimd.tensor_tensor(parts[:, k, 2, :], rest[:, k % 2, :], parts[:, k, 1, :],
                                            ALU.subtract).then_inc(s_p3, 1)
            pool.wait_ge(s_vev, 2 * B)

            def unit(b, g, first):
                w = UNITS * b + g
                if not first:
                    pool.wait_ge(s_pv, T * (w - UNITS + 1))
                nc.gpsimd.tensor_tensor(
                    v_st[:, g, :, :, 0:HD],
                    v_all[:, bass.ts(b, T), G * HD * g:G * HD * (g + 1)].rearrange("p t (j d) -> p t j d", j=G),
                    zeros[:, :].rearrange("p (t j d) -> p t j d", t=T, j=G), ALU.add).then_inc(s_vst, 1)
                pool.wait_ge(s_red, 2 * T * (w + 1))
                if not (first and g < 2):
                    pool.wait_ge(s_mt, w - 1)
                src = neg_max[:, g, :, :].rearrange("p j t -> p (j t)")
                mp, mr = m_parts[:, g % 2], m_rest[:, :, :]
                nc.gpsimd.tensor_tensor(mp[:, 0, :], src, zeros[:, 0:G * T], ALU.add).then_inc(s_mstep, 1)
                pool.wait_ge(s_mstep, 4 * w + 1)
                nc.gpsimd.tensor_tensor(mr[:, 0, :], src, mp[:, 0, :], ALU.subtract).then_inc(s_mstep, 1)
                pool.wait_ge(s_mstep, 4 * w + 2)
                nc.gpsimd.tensor_tensor(mp[:, 1, :], mr[:, 0, :], zeros[:, 0:G * T], ALU.add).then_inc(s_mstep, 1)
                pool.wait_ge(s_mstep, 4 * w + 3)
                nc.gpsimd.tensor_tensor(mp[:, 2, :], mr[:, 0, :], mp[:, 1, :], ALU.subtract).then_inc(s_mstep, 1)
                pool.wait_ge(s_mstep, 4 * w + 4)
                pool.sem_inc(s_mp, 1)

            for g in range(UNITS):
                unit(0, g, True)
            with pool.Fori(1, B) as b:
                for g in range(UNITS):
                    unit(b, g, False)
            with pool.Fori(0, B // 2) as i:
                for par in range(2):
                    b = 2 * i + par
                    pool.wait_ge(s_rr, 2 * DMA * (b + 1))
                    pool.wait_ge(s_ds, 2 * DMA * UNITS * (b + 1))
                    pool.wait_ge(s_fc, 4 * i)
                    for half in range(2):
                        nc.gpsimd.tensor_tensor(ctxT[:, par, half, :], heads_out[:, half, bass.ts(b, S)],
                                                r_all[:, half, bass.ts(b, S)], ALU.mult).then_inc(s_ct, 1)

        @block.scalar
        def _(act):
            def sqrt_var(b):
                for n in range(2):
                    act.wait_ge(s_mv, 2 * b + n + 1)
                    nc.scalar.activation(std[:, bass.ts(n, T)], mv[:, bass.ts(n, T), 1], ACT.Sqrt,
                                         bias=eps[:, 0:1]).then_inc(s_sd, 1)

            def transposed_inputs(b, trn):
                for n in range(3):
                    for f in range(FT):
                        k = FT * min(n, 1) + f
                        act.wait_ge(s_tr, 4 * b + k + 1)
                        if f == 0:
                            if n < 2:
                                act.wait_ge(s_prj, 4 * b)
                            else:
                                act.wait_ge(s_vprj, 2 * b)
                        nc.scalar.activation(lnT[:, n, f, :], trn[k], ACT.Identity,
                                             scale=lnc[:, 2 * n, f:f + 1], bias=lnc[:, 2 * n + 1, f:f + 1])\
                          .then_inc(s_tev, 1)

            def first_parts(b, prj):
                for k in range(4):
                    act.wait_ge(s_prj, 4 * b + k + 1)
                    act.wait_ge(s_pw[k], 3 * DMA * b)
                    nc.scalar.activation(parts[:, k, 0, :], prj[k], ACT.Identity).then_inc(s_p1, 1)

            def values(b, vps):
                for k in range(2):
                    act.wait_ge(s_vprj, 2 * b + k + 1)
                    nc.scalar.activation(v_all[:, bass.ds(b * T + 2 * k, 2)],
                                         vps[k].rearrange("p (t n) -> p t n", t=2), ACT.Identity)\
                      .then_inc(s_vev, 1)

            act.wait_ge(s_eps, 1)
            sqrt_var(0)
            act.wait_ge(s_cst, 2 * DMA)
            with act.Fori(0, B - 1) as i:
                transposed_inputs(i, trn)
                sqrt_var(i + 1)
                first_parts(i, prj)
                values(i, vps)
            transposed_inputs(B - 1, trn_last)
            first_parts(B - 1, prj_last)
            values(B - 1, vps_last)

            def max_rows(b, slot, par):
                act.wait_ge(s_mt, UNITS * b + slot + 1)
                nc.scalar.activation(m_rows[:, par, :], mt_ps[0:MROWS * G * T, :], ACT.Identity)\
                  .then_inc(s_mtev, 1)

            def unit_output(b, g):
                u = UNITS * b + g
                act.wait_ge(s_pv, T * (u + 1))
                act.wait_ge(s_ow[g % 2], DMA * (2 * b + g // 2))
                nc.scalar.activation(o_sb[:, g % 2, :], pv_ps, ACT.Identity).then_inc(s_oev, 1)

            def batch(b, last):
                for g in range(UNITS):
                    for s in range(TILES):
                        q, m = T * g + s // G, TILES * g + s
                        act.wait_ge(s_st, TILES * UNITS * b + m + 1)
                        if s % G == 0:
                            act.wait_ge(s_pv, T * UNITS * b + max(q - 3, 0))
                        nc.scalar.activation(probs[:, q % 4, s % G, :], st_ps[m % 2], ACT.Exp, scale=SCALE)\
                          .then_inc(s_exp, 1)
                        if s == 3 and g:
                            unit_output(b, g - 1)
                        if s == 11 and not (last and g == UNITS - 1):
                            if g:
                                act.wait_ge(s_mrow[g - 1], DMA * (b + 1))
                            else:
                                act.wait_ge(s_mrow[UNITS - 1], DMA * b)
                            max_rows(b, g + 1, (g + 1) % 2)
                unit_output(b, UNITS - 1)

            nc.scalar.activation(warm[:, :], eps[:, :], ACT.Exp).then_inc(s_warm, 1)
            max_rows(0, 0, 0)
            with act.Fori(0, B - 1) as b:
                batch(b, False)
            batch(B - 1, True)

        @block.vector
        def _(dve):
            def statistics(b, n):
                dve.wait_ge((s_lx, s_lc)[n], DMA * (b + 1))
                for t in range(T):
                    row = (xin, cin)[n][:, bass.ds(b * T + t, 1), :].rearrange("p a d -> p (a d)")
                    last = nc.vector.bn_stats(stats[:, n * T + t, :], row)
                last.then_inc(s_bs, 1)
                wait_alone(dve, "dve", s_bs, 2 * b + n + 1)
                for t in range(T):
                    last = nc.vector.bn_aggr(mv[:, n * T + t, :], stats[:, n * T + t, :])
                last.then_inc(s_mv, 1)

            def inverse_std(own, done):
                y, y2, vy2, corr = (newton[:, k, own] for k in range(4))
                nc.vector.reciprocal(y, std[:, own]).then_inc(s_nw, 1)
                dve.wait_ge(s_nw, done + 1)
                nc.vector.tensor_tensor(y2, y, y, ALU.mult).then_inc(s_nw, 1)
                dve.wait_ge(s_nw, done + 2)
                nc.vector.scalar_tensor_tensor(out=vy2, in0=mv[:, own, 1], scalar=EPS, in1=y2,
                                               op0=ALU.add, op1=ALU.mult).then_inc(s_nw, 1)
                dve.wait_ge(s_nw, done + 3)
                nc.vector.tensor_scalar(corr, vy2, -0.5, 1.5, ALU.mult, ALU.add).then_inc(s_nw, 1)
                dve.wait_ge(s_nw, done + 4)
                nc.vector.tensor_tensor(rstd[:, own], y, corr, ALU.mult).then_inc(s_nw, 1)
                dve.wait_ge(s_nw, done + 5)

            def normalise(b, n):
                dve.wait_ge(s_tr, 4 * b)
                for t in range(T):
                    k = n * T + t
                    row = (xin, cin)[n][:, bass.ds(b * T + t, 1), :].rearrange("p a d -> p (a d)")
                    last = nc.vector.tensor_scalar(xn[:, n, t, :], row, mv[:, k, 0:1], rstd[:, k:k + 1],
                                                   ALU.subtract, ALU.mult)
                last.then_inc(s_xn, 1)

            def second_part(b, k, prj):
                dve.wait_ge(s_p1, 4 * b + k + 1)
                dve.wait_ge(s_p3, 4 * b + max(k - 1, 0))
                nc.vector.tensor_tensor(rest[:, k % 2, :], prj[k], parts[:, k, 0, :], ALU.subtract)\
                  .then_inc(s_rest, 1)
                dve.wait_ge(s_rest, 4 * b + k + 1)
                nc.vector.tensor_copy(parts[:, k, 1, :], rest[:, k % 2, :]).then_inc(s_p2, 1)

            def max_pair(b, g, k):
                t, h = k // 2, k % 2
                dve.wait_ge(s_mx, 2 * T * (UNITS * b + g) + k + 1)
                nc.vector.tensor_reduce(neg_max[:, g, 2 * h:2 * h + 2, t], mx_ps[h], AX.X, ALU.max,
                                        negate=True).then_inc(s_red, 1)

            nc.vector.memset(eps[:, :], EPS).then_inc(s_eps, 1)
            for n in range(2):
                statistics(0, n)
                dve.wait_ge(s_sd, n + 1)
                inverse_std(bass.ts(n, T), 5 * n)
                normalise(0, n)
            dve.wait_ge(s_cst, 2 * DMA)
            nc.vector.tensor_copy(ident_b[:, :], ident[:, :]).then_inc(s_ib, 1)
            with dve.Fori(0, B - 1) as i:
                for n in range(2):
                    statistics(i + 1, n)
                second_part(i, 0, prj)
                dve.wait_ge(s_sd, 2 * i + 4)
                inverse_std(slice(0, 2 * T), 5 * i + 10)
                second_part(i, 1, prj)
                normalise(i + 1, 0)
                second_part(i, 2, prj)
                second_part(i, 3, prj)
                normalise(i + 1, 1)
            for k in range(2):
                max_pair(0, 0, k)
            for k in range(4):
                second_part(B - 1, k, prj_last)
                max_pair(0, 0, 2 + k)
            for k in range(6, 2 * T):
                max_pair(0, 0, k)

            def recip(b):
                dve.wait_ge(s_ds, 2 * DMA * UNITS * (b + 1))
                nc.vector.reciprocal(recips[:, b, :], sums[:, b, :]).then_inc(s_rc, 1)

            for g in range(1, UNITS):
                for k in range(2 * T):
                    max_pair(0, g, k)
            with dve.Fori(1, B) as b:
                for g in range(UNITS):
                    dve.wait_ge(s_mp, UNITS * b + g - UNITS + 1)
                    for k in range(2 * T):
                        max_pair(b, g, k)
                    if g == 2:
                        recip(b - 1)
            recip(B - 1)
            with dve.Fori(0, B // 2) as i:
                for par in range(2):
                    for h in range(2):
                        k = 2 * par + h
                        dve.wait_ge(s_fc, 4 * i + k + 1)
                        dve.wait_ge(s_xr, B)
                        dst = xin[:, bass.ds(i * 2 * T + 2 * k, 2)]
                        nc.vector.tensor_tensor(dst, ps[:, k, :].rearrange("p (t n) -> p t n", t=2), dst, ALU.add)\
                          .then_inc(s_fin, 1)

        @block.tensor
        def _(pe):
            def transposes(b, trn):
                for n in range(2):
                    pe.wait_ge(s_xn, 2 * b + n + 1)
                    for f in range(FT):
                        for t in range(T):
                            last = nc.tensor.transpose(trn[FT * n + f][:, bass.ts(t, P)],
                                                       xn[:, n, t, bass.ts(f, P)], ident[:, :])
                        last.then_inc(s_tr, 1)

            def projection(b, k, bank):
                n, half = k // 2, k % 2
                for f in range(FT):
                    last = nc.tensor.matmul(bank, w_sb["qk"[n]][:, f, bass.ts(half, P)], lnT[:, n, f, :],
                                            start=(f == 0), stop=(f == FT - 1))
                last.then_inc(s_prj, 1)

            def values(k, bank):
                for h in range(2):
                    for f in range(FT):
                        last = nc.tensor.matmul(bank[:, bass.ts(h, DM)], lnT[:, 2, f, bass.ts(2 * k + h, P)],
                                                w_sb["v"][:, f, :], start=(f == 0), stop=(f == FT - 1))
                last.then_inc(s_vprj, 1)

            def max_tile(b, n):
                g, t, j = n // TILES, n % TILES // G, n % G
                b, g = b + g // UNITS, g % UNITS
                if n % TILES == 0:
                    pe.wait_ge(s_load[g], 2 * DMA * (b + 1))
                if j % 2 == 0 and not (isinstance(b, int) and b == 0 and n < 4):
                    pe.wait_ge(s_red, (TILES * UNITS * b + n % (TILES * UNITS)) // 2 - 1 if isinstance(b, int)
                               else TILES * UNITS // 2 * b + n % (TILES * UNITS) // 2 - 1)
                r = nc.tensor.matmul(mx_ps[j // 2][:, j % 2, :], qs[0:ROWS, g, j, bass.ts(t, P)], ks[0:ROWS, g, j, :],
                                     start=True, stop=True)
                if j % 2:
                    r.then_inc(s_mx, 1)

            def max_transpose(b, slot, par):
                w = UNITS * b + slot
                pe.wait_ge(s_mp, w + 1)
                wait_alone(pe, "pe", s_mtev, w)
                nc.tensor.transpose(mt_ps[0:MROWS * G * T, :], m_parts[:, par].rearrange("p c n -> p (c n)"),
                                    ident_b[:, :]).then_inc(s_mt, 1)

            def score_tile(b, m):
                g, t, j = m // TILES, m % TILES // G, m % G
                if m % TILES == 0:
                    pe.wait_ge(s_mrow[g], DMA * (b + 1))
                if m > 1:
                    pe.wait_ge(s_exp, TILES * UNITS * b + m - 1)
                elif m == 0:
                    pe.wait_ge(s_exp, TILES * UNITS * b)
                nc.tensor.matmul(st_ps[m % 2], ks[0:ROWS + MROWS, g, j, bass.ts(t, P)], qs[0:ROWS + MROWS, g, j, :],
                                 start=True, stop=True).then_inc(s_st, 1)

            def values_product(b, q, half):
                g, t = q // T, q % T
                u = UNITS * b + g
                if half == 0:
                    if t == 0:
                        pe.wait_ge(s_vst, u + 1)
                        pe.wait_ge(s_oev, u)
                    pe.wait_ge(s_exp, TILES * UNITS * b + G * (q + 1))
                own = bass.ts(half, S // 2)
                for j in range(G):
                    last = nc.tensor.matmul(pv_ps[32 * j:32 * j + 32, own], v_st[:, g, t, j, :],
                                            probs[:, q % 4, j, own], start=(t == 0 and half == 0),
                                            stop=(t == T - 1 and half == 1), skip_group_check=True)
                if half:
                    last.then_inc(s_pv, 1)

            def batch(b, last):
                for q in range(T * UNITS):
                    score, bound = G * q, TILES * UNITS if last else 2 * TILES * UNITS
                    for half in range(2):
                        for j in (2 * half, 2 * half + 1):
                            score_tile(b, score + j)
                            if score + j + LEAD < bound:
                                max_tile(b, score + j + LEAD)
                        if half and q % T == T - 2 and not (last and q > T * UNITS - T):
                            max_transpose(b, q // T + 1, (q // T + 1) % 2)
                        if q:
                            values_product(b, q - 1, half)
                for half in range(2):
                    values_product(b, T * UNITS - 1, half)

            pe.wait_ge(s_cst, 2 * DMA)
            with pe.Fori(0, B - 1) as i:
                pe.wait_ge(s_tev, 6 * i)
                transposes(i, trn)
                pe.wait_ge(s_w, 5 * DMA)
                for k in range(4):
                    pe.wait_ge(s_tev, 6 * i + 2 * (k // 2) + 2)
                    pe.wait_ge(s_rest, 4 * i + max(k - 1, 0))
                    projection(i, k, prj[k])
                pe.wait_ge(s_tev, 6 * i + 6)
                pe.wait_ge(s_vev, 2 * i)
                for k in range(2):
                    values(k, vps[k])

            done = B - 1
            pe.wait_ge(s_tev, 6 * done)
            pe.wait_ge(s_vev, 2 * done)
            transposes(done, trn_last)
            pe.wait_ge(s_rest, 4 * done)
            pe.wait_ge(s_ones, 1)
            for n in range(4):
                max_tile(0, n)
            for k in range(4):
                pe.wait_ge(s_tev, 6 * done + (2, 2, 6, 6)[k])
                projection(done, k, prj_last[k])
                max_tile(0, 4 + 2 * k)
                max_tile(0, 5 + 2 * k)
            pe.wait_ge(s_rest, 4 * done + 2)
            for k in range(2):
                values(k, vps_last[k])
                max_tile(0, 12 + 2 * k)
                max_tile(0, 13 + 2 * k)
            pe.wait_ge(s_rest, 4 * B)
            pe.wait_ge(s_vev, 2 * B)
            pe.wait_ge(s_vones, 1)
            pe.wait_ge(s_ib, 1)
            for n in range(16, LEAD):
                if n == 24:
                    max_transpose(0, 0, 0)
                max_tile(0, n)
            with pe.Fori(0, B - 1) as b:
                batch(b, False)
            batch(B - 1, True)

            pe.wait_ge(s_oev, B * UNITS)
            with pe.Fori(0, B // 2) as i:
                for par in range(2):
                    pe.wait_ge(s_ct, 4 * i + 2 * par + 2)
                    if par == 0:
                        pe.wait_ge(s_fin, 4 * i)
                    for t in range(T):
                        for half in range(2):
                            last = nc.tensor.matmul(ps[:, 2 * par + t // 2, bass.ts(t % 2, DM)],
                                                    ctxT[:, par, half, bass.ts(t, P)], w_sb["fc"][:, half, :],
                                                    start=(half == 0), stop=(half == 1))
                        if t % 2:
                            last.then_inc(s_fc, 1)


def kernel(x, ctx_1024, L0_xattn_ln_q_g, L0_xattn_ln_q_b, L0_xattn_ln_k_g, L0_xattn_ln_k_b, L0_xattn_ln_v_g,
           L0_xattn_ln_v_b, L0_xattn_w_q, L0_xattn_w_k, L0_xattn_w_v, L0_xattn_w_fc, L0_xattn_b_fc):
    import numpy as np
    import concourse.bacc as bacc
    from concourse.bass_utils import run_bass_kernel_spmd

    def by_dimension(w):
        return np.ascontiguousarray(np.asarray(w).T.reshape(DM, 2, HEADS // 2, HD).transpose(0, 1, 3, 2)
                                    .reshape(DM, DM))

    vectors = (L0_xattn_ln_q_g, L0_xattn_ln_q_b, L0_xattn_ln_k_g, L0_xattn_ln_k_b, L0_xattn_ln_v_g, L0_xattn_ln_v_b)
    arrays = {
        "x": np.asarray(x),
        "context": np.asarray(ctx_1024),
        "wqT": by_dimension(L0_xattn_w_q),
        "wkT": by_dimension(L0_xattn_w_k),
        "wvT": np.ascontiguousarray(np.asarray(L0_xattn_w_v).T),
        "wfcT": np.ascontiguousarray(np.asarray(L0_xattn_w_fc).T),
        "ln_cols": np.ascontiguousarray(np.stack([np.asarray(v).reshape(FT, P) for v in vectors]).transpose(2, 0, 1)),
        "b_fc": np.asarray(L0_xattn_b_fc),
        "eye": np.eye(P, dtype=np.float32),
    }
    nc = bacc.Bacc("TRN2", target_bir_lowering=False, num_devices=1)
    args = [nc.dram_tensor(n, a.shape, mybir.dt.from_np(a.dtype), kind="ExternalInput").ap()
            for n, a in arrays.items()]
    out = nc.dram_tensor("out", (B, S, DM), F32, kind="ExternalOutput").ap()
    build(nc, *args, out)
    result = run_bass_kernel_spmd(nc, [arrays], core_ids=[0])
    return result.results[0]["out"]
```

```python
from contextlib import ExitStack

import concourse.bass as bass
from concourse import mybir

F32 = mybir.dt.float32
BF16 = mybir.dt.bfloat16
ALU = mybir.AluOpType
ACT = mybir.ActivationFunctionType
AX = mybir.AxisListType

P = 128
B, S, DM = 4, 512, 256
HEADS, HD = 16, 16
G = 4
UNITS = HEADS // G
T = S // P
FT = DM // P
ROWS = 6 * HD
MROWS = 3
TILES = T * G
QUADS = T * UNITS
LEAD = 24
EPS = 1e-5
SCALE = float(HD) ** -0.5
QPARTS = ((0, 0, 3), (3, 1, 2), (5, 2, 1))
DMA = 16


def build(nc, x, ctx_in, wq, wk, wv, wfc, ln_cols, b_fc, eye, out):
    with ExitStack() as stack:
        def sb(name, shape, dt=F32):
            return stack.enter_context(nc.sbuf_tensor(name, shape, dt))

        def sem(name):
            return stack.enter_context(nc.semaphore(name))

        q_rows = nc.dram_tensor("q_rows", (B, 2, 6, HD, HEADS // 2, S), BF16, kind="Internal").ap()
        k_rows = nc.dram_tensor("k_rows", (B, 2, 6, HD, HEADS // 2, S), BF16, kind="Internal").ap()
        unit_out = nc.dram_tensor("unit_out", (B, UNITS, G, 32, S), F32, kind="Internal").ap()
        recip_rows = nc.dram_tensor("recip_rows", (B, HEADS, S), F32, kind="Internal").ap()

        ident = sb("ident", [P, P])
        ident_b = sb("ident_b", [P, P], BF16)
        w_sb = {n: sb("w_" + n, [P, FT, DM]) for n in ("q", "k", "v", "fc")}
        lnc = sb("lnc", [P, 6, FT])
        bias = sb("bias", [P, DM])
        eps = sb("eps", [P, 1])
        warm = sb("warm", [P, 1])
        heat = sb("heat", [P, S], BF16)
        xin = sb("xin", [P, B * T, DM])
        cin = sb("cin", [P, B * T, DM])
        xn = sb("xn", [P, 2, T, DM])
        stats = sb("stats", [P, 2 * T, 6])
        mv = sb("mv", [P, 2 * T, 2])
        std = sb("std", [P, 2 * T])
        newton = sb("newton", [P, 4, 2 * T])
        rstd = sb("rstd", [P, 2 * T])
        lnT = sb("lnT", [P, 3, FT, S])
        parts = sb("parts", [P, 4, 3, S], BF16)
        rest = sb("rest", [P, 2, S])
        v_all = sb("v_all", [P, B * T, DM])
        qs = sb("qs", [P, UNITS, G, S], BF16)
        ks = sb("ks", [P, UNITS, G, S], BF16)
        neg_max = sb("neg_max", [P, 4, G, T])
        m_rest = sb("m_rest", [P, 2, G * T])
        m_parts = sb("m_parts", [P, 2, MROWS, G * T], BF16)
        m_rows = sb("m_rows", [MROWS * G * T, 2, P], BF16)
        v_st = sb("v_st", [P, UNITS, T, G, 32])
        zeros = sb("zeros", [P, T * G * HD])
        probs = sb("probs", [P, 4, G, S])
        o_sb = sb("o_sb", [P, 2, S])
        heads_out = cin[:, :, :].rearrange("p a b -> p (a b)").rearrange("p (h t) -> p h t", h=2)
        sums = sb("sums", [P, B, S // 8])
        recips = sb("recips", [P, B, S // 8])
        r_all = sb("r_all", [P, 2, B * S])
        ctxT = sb("ctxT", [P, 2, 2, S])

        ps = stack.enter_context(nc.psum_tensor("ps", [P, 8, S], F32))
        trn = [ps[:, k] for k in (0, 1, 2, 3)]
        prj = [ps[:, k] for k in (4, 5, 6, 7)]
        vps, vps_last = [ps[:, k] for k in (4, 5)], [ps[:, k] for k in (0, 1)]
        st_ps = [ps[:, k] for k in range(2)]
        mx_ps = [ps[:, 2 + 2 * k:4 + 2 * k] for k in range(2)]
        pv_ps = ps[:, 6]
        mt_ps = ps[:, 7, 0:P // 2].bitcast(BF16)

        s_x01, s_lx, s_lc, s_cst, s_wq, s_w = (sem("s_x01"), sem("s_lx"), sem("s_lc"), sem("s_cst"), sem("s_wq"),
                                               sem("s_w"))
        s_ib, s_eps = sem("s_ib"), sem("s_eps")
        s_bs, s_mv, s_sd, s_nw, s_xn = sem("s_bs"), sem("s_mv"), sem("s_sd"), sem("s_nw"), sem("s_xn")
        s_tr, s_tev, s_prj, s_vprj, s_vev = sem("s_tr"), sem("s_tev"), sem("s_prj"), sem("s_vprj"), sem("s_vev")
        s_p1, s_rest, s_p2, s_p3, s_xr = sem("s_p1"), sem("s_rest"), sem("s_p2"), sem("s_p3"), sem("s_xr")
        s_pw = [sem(f"s_pw{k}") for k in range(4)]
        s_load = [sem(f"s_load{g}") for g in range(UNITS)]
        s_mrow = [sem(f"s_mrow{g}") for g in range(UNITS)]
        s_ones, s_vones = sem("s_ones"), sem("s_vones")
        s_mx, s_red, s_mstep, s_mp, s_mt, s_mtev = (sem("s_mx"), sem("s_red"), sem("s_mstep"), sem("s_mp"),
                                                    sem("s_mt"), sem("s_mtev"))
        s_st, s_exp, s_vst, s_pv, s_oev = sem("s_st"), sem("s_exp"), sem("s_vst"), sem("s_pv"), sem("s_oev")
        s_ow = [sem(f"s_ow{k}") for k in range(2)]
        s_ds, s_rc, s_rw, s_rr = sem("s_ds"), sem("s_rc"), sem("s_rw"), sem("s_rr")
        s_ct, s_fc, s_fin, s_out = sem("s_ct"), sem("s_fc"), sem("s_fin"), sem("s_out")

        x_t = x.rearrange("b (t p) d -> b p t d", p=P)
        c_t = ctx_in.rearrange("b (t p) d -> b p t d", p=P)
        out_t = out.rearrange("b (t p) d -> b p t d", p=P)

        s_zero, s_warm, s_heat = sem("s_zero"), sem("s_warm"), sem("s_heat")
        s_own = {e: sem("s_own_" + e) for e in ("sp", "dve", "pe")}

        def wait_alone(eng, name, semaphore, value):
            eng.wait_ge(semaphore, value)
            eng.sem_inc(s_own[name], 1)

        block = stack.enter_context(nc.Block())

        @block.sync
        def _(sp):
            def load_inputs(b):
                sp.dma_start(xin[:, bass.ts(b, T)], x_t[b]).then_inc(s_lx, DMA)
                sp.dma_start(cin[:, bass.ts(b, T)], c_t[b]).then_inc(s_lc, DMA)

            def write_parts(b):
                for k in range(4):
                    wait_alone(sp, "sp", s_p3, 4 * b + k + 1)
                    if k < 2:
                        for row, part, n in QPARTS:
                            dst = q_rows[b, k % 2, row:row + n].rearrange("c d h t -> (d h) c t")
                            src = parts[:, k, part, :].unsqueeze(1).to_broadcast([P, n, S])
                            sp.dma_start(dst, src).then_inc(s_pw[k], DMA)
                    else:
                        for row, n in ((0, 3), (3, 2), (5, 1)):
                            dst = k_rows[b, k % 2, row:row + n].rearrange("c d h t -> (d h) c t")
                            sp.dma_start(dst, parts[:, k, 0:n, :]).then_inc(s_pw[k], DMA)

            def load_stacks(b, g):
                wait_alone(sp, "sp", s_pw[g // 2], 3 * DMA * (b + 1))
                wait_alone(sp, "sp", s_pw[2 + g // 2], 3 * DMA * (b + 1))
                for rows, dst in ((q_rows, qs), (k_rows, ks)):
                    sp.dma_start(dst[0:ROWS, g], rows[b, g // 2, :, :, bass.ts(g % 2, G)].rearrange("c d h t -> (c d) h t"))\
                      .then_inc(s_load[g], DMA)

            def write_max_rows(w, slot, par):
                wait_alone(sp, "sp", s_mtev, w + 1)
                sp.dma_start(qs[ROWS:ROWS + MROWS, slot], m_rows[:, par, :]).then_inc(s_mrow[slot], DMA)

            def store_unit(b, g):
                u = UNITS * b + g
                wait_alone(sp, "sp", s_oev, u + 1)
                sp.dma_start(unit_out[b, g].rearrange("j r t -> (j r) t"), o_sb[:, g % 2, :])\
                  .then_inc(s_ow[g % 2], DMA)
                wait_alone(sp, "sp", s_ow[g % 2], DMA * (2 * b + g // 2 + 1))
                wait_alone(sp, "sp", s_ds, 2 * DMA * u)
                rows = 64 * (g % 2)
                sp.dma_start(heads_out[rows:rows + 64, g // 2, bass.ts(b, S)], unit_out[b, g, :, 0:HD, :])\
                  .then_inc(s_ds, DMA)
                sp.dma_start(sums[32 * g:32 * g + 32, b, :],
                             unit_out[b, g, :, HD, :].rearrange("j (c w) -> j c w", c=8)).then_inc(s_ds, DMA)

            def spread_recips(b):
                wait_alone(sp, "sp", s_rc, b + 1)
                sp.dma_start(recip_rows[b].rearrange("h (c w) -> (h c) w", c=8), recips[:, b, :])\
                  .then_inc(s_rw, DMA)
                wait_alone(sp, "sp", s_rw, DMA * (b + 1))
                wait_alone(sp, "sp", s_rr, 2 * DMA * b)
                for half in range(2):
                    src = recip_rows[b, bass.ts(half, HEADS // 2), :].unsqueeze(1)\
                        .to_broadcast([HEADS // 2, HD, S])
                    sp.dma_start(r_all[:, half, bass.ts(b, S)], src).then_inc(s_rr, DMA)

            def batch(b, first=False, last=False):
                for g in range(UNITS):
                    if g and not last:
                        wait_alone(sp, "sp", s_st, TILES * (UNITS * b + g))
                        load_stacks(b + 1, g - 1)
                    if g:
                        store_unit(b, g - 1)
                    if not (last and g == UNITS - 1):
                        write_max_rows(UNITS * b + g + 1, (g + 1) % UNITS, (g + 1) % 2)
                if not first:
                    spread_recips(b - 1)
                if not last:
                    wait_alone(sp, "sp", s_st, TILES * UNITS * (b + 1))
                    load_stacks(b + 1, UNITS - 1)
                store_unit(b, UNITS - 1)

            sp.dma_start(xin[:, 0:2], x_t[0][:, 0:2]).then_inc(s_x01, DMA)
            sp.dma_start(xin[:, 2:T], x_t[0][:, 2:T]).then_inc(s_lx, DMA)
            sp.dma_start(ident[:, :], eye).then_inc(s_cst, DMA)
            sp.dma_start(lnc[:, :, :], ln_cols).then_inc(s_cst, DMA)
            sp.dma_start(w_sb["q"][:, :, :], wq.rearrange("(f p) n -> p f n", p=P)).then_inc(s_wq, DMA)
            sp.dma_start(cin[:, 0:T], c_t[0]).then_inc(s_lc, DMA)
            for n, w in (("k", wk), ("v", wv), ("fc", wfc)):
                sp.dma_start(w_sb[n][:, :, :], w.rearrange("(f p) n -> p f n", p=P)).then_inc(s_w, DMA)
            sp.dma_start(bias[:, :], b_fc.partition_broadcast(P)).then_inc(s_w, DMA)
            with sp.Fori(1, B) as i:
                wait_alone(sp, "sp", s_lx, DMA * i)
                wait_alone(sp, "sp", s_lc, DMA * i)
                load_inputs(i)
            write_parts(0)
            load_stacks(0, 0)
            load_stacks(0, 1)
            with sp.Fori(1, B - 1) as i:
                write_parts(i)
            load_stacks(0, 2)
            write_parts(B - 1)
            write_max_rows(0, 0, 0)
            load_stacks(0, 3)
            batch(0, first=True)
            with sp.Fori(1, B - 1) as b:
                batch(b)
            batch(B - 1, last=True)
            spread_recips(B - 1)
            with sp.Fori(0, B) as b:
                for h in range(2):
                    wait_alone(sp, "sp", s_fin, 2 * b + h + 1)
                    sp.dma_start(out_t[b][:, bass.ts(h, 2)], xin[:, bass.ds(b * T + 2 * h, 2)])\
                      .then_inc(s_out, DMA)
            wait_alone(sp, "sp", s_out, DMA * 2 * B)

        @block.gpsimd
        def _(pool):
            nc.gpsimd.memset(ks[ROWS:P, :, :, :], 1.0).then_inc(s_ones, 1)
            pool.wait_ge(s_ones, 1)
            nc.gpsimd.memset(v_st[:, :, :, :, HD:32], 1.0).then_inc(s_vones, 1)
            nc.gpsimd.memset(zeros[:, :], 0.0).then_inc(s_zero, 1)
            pool.wait_ge(s_zero, 1)
            pool.wait_ge(s_w, 4 * DMA)
            def third_parts(b):
                for k in range(4):
                    pool.wait_ge(s_p2, 4 * b + k + 1)
                    nc.gpsimd.tensor_tensor(parts[:, k, 2, :], rest[:, k % 2, :], parts[:, k, 1, :],
                                            ALU.subtract).then_inc(s_p3, 1)

            def add_bias(b):
                pool.wait_ge(s_xn, 2 * b + 1)
                nc.gpsimd.tensor_tensor(xin[:, bass.ts(b, T)], xin[:, bass.ts(b, T)],
                                        bias[:, :].unsqueeze(1).to_broadcast([P, T, DM]), ALU.add)\
                  .then_inc(s_xr, 1)

            def minus_max_parts(b, g, first=False):
                w = UNITS * b + g
                pool.wait_ge(s_red, 2 * T * (w + 1))
                if not (first and g < 2):
                    pool.wait_ge(s_mt, w - 1)
                src = neg_max[:, g, :, :].rearrange("p j t -> p (j t)")
                mp, mr = m_parts[:, g % 2], m_rest[:, :, :]
                nc.gpsimd.tensor_tensor(mp[:, 0, :], src, zeros[:, 0:G * T], ALU.add).then_inc(s_mstep, 1)
                pool.wait_ge(s_mstep, 4 * w + 1)
                nc.gpsimd.tensor_tensor(mr[:, 0, :], src, mp[:, 0, :], ALU.subtract).then_inc(s_mstep, 1)
                pool.wait_ge(s_mstep, 4 * w + 2)
                nc.gpsimd.tensor_tensor(mp[:, 1, :], mr[:, 0, :], zeros[:, 0:G * T], ALU.add).then_inc(s_mstep, 1)
                pool.wait_ge(s_mstep, 4 * w + 3)
                nc.gpsimd.tensor_tensor(mp[:, 2, :], mr[:, 0, :], mp[:, 1, :], ALU.subtract).then_inc(s_mstep, 1)
                pool.wait_ge(s_mstep, 4 * w + 4)
                pool.sem_inc(s_mp, 1)

            def stage_values(b, g, first=False):
                w = UNITS * b + g
                if not first:
                    pool.wait_ge(s_pv, T * (w - UNITS + 1))
                nc.gpsimd.tensor_tensor(
                    v_st[:, g, :, :, 0:HD],
                    v_all[:, bass.ts(b, T), G * HD * g:G * HD * (g + 1)].rearrange("p t (j d) -> p t j d", j=G),
                    zeros[:, :].rearrange("p (t j d) -> p t j d", t=T, j=G), ALU.add).then_inc(s_vst, 1)

            with pool.Fori(0, B - 1) as i:
                third_parts(i)
                add_bias(i)
            third_parts(B - 1)
            minus_max_parts(0, 0, first=True)
            pool.wait_ge(s_vev, 2 * B)
            stage_values(0, 0, first=True)
            add_bias(B - 1)
            for g in range(1, UNITS):
                minus_max_parts(0, g, first=True)
                stage_values(0, g, first=True)
            with pool.Fori(1, B) as b:
                for g in range(UNITS):
                    minus_max_parts(b, g)
                    stage_values(b, g)
            with pool.Fori(0, B // 2) as i:
                for par in range(2):
                    b = 2 * i + par
                    pool.wait_ge(s_rr, 2 * DMA * (b + 1))
                    pool.wait_ge(s_ds, 2 * DMA * UNITS * (b + 1))
                    pool.wait_ge(s_fc, 4 * i)
                    for half in range(2):
                        nc.gpsimd.tensor_tensor(ctxT[:, par, half, :], heads_out[:, half, bass.ts(b, S)],
                                                r_all[:, half, bass.ts(b, S)], ALU.mult).then_inc(s_ct, 1)

        @block.scalar
        def _(act):
            def sqrt_var(b, which=(0, 1)):
                for n in which:
                    act.wait_ge(s_mv, 2 * b + n + 1)
                    nc.scalar.activation(std[:, bass.ts(n, T)], mv[:, bass.ts(n, T), 1], ACT.Sqrt,
                                         bias=eps[:, 0:1]).then_inc(s_sd, 1)

            def transposed(b, n):
                for f in range(FT):
                    k = FT * min(n, 1) + f
                    act.wait_ge(s_tr, 4 * b + k + 1)
                    nc.scalar.activation(lnT[:, n, f, :], trn[k], ACT.Identity,
                                         scale=lnc[:, 2 * n, f:f + 1], bias=lnc[:, 2 * n + 1, f:f + 1])\
                      .then_inc(s_tev, 1)

            def first_parts(b, own):
                for k in own:
                    act.wait_ge(s_prj, 4 * b + k + 1)
                    act.wait_ge(s_pw[k], 3 * DMA * b)
                    nc.scalar.activation(parts[:, k, 0, :], prj[k], ACT.Identity).then_inc(s_p1, 1)

            def second_parts(b, own):
                for k in own:
                    act.wait_ge(s_rest, 4 * b + k + 1)
                    nc.scalar.activation(parts[:, k, 1, :], rest[:, k % 2, :], ACT.Identity).then_inc(s_p2, 1)

            def values(b, k, vps):
                act.wait_ge(s_vprj, 2 * b + k + 1)
                nc.scalar.activation(v_all[:, bass.ds(b * T + 2 * k, 2)],
                                     vps[k].rearrange("p (t n) -> p t n", t=2), ACT.Identity)\
                  .then_inc(s_vev, 1)

            act.wait_ge(s_eps, 1)
            nc.scalar.activation(warm[:, :], eps[:, :], ACT.Sqrt).then_inc(s_warm, 1)
            sqrt_var(0, (0,))
            act.wait_ge(s_cst, 2 * DMA)
            transposed(0, 0)
            sqrt_var(0, (1,))
            transposed(0, 1)
            transposed(0, 2)
            with act.Fori(0, B - 1) as i:
                first_parts(i, (0, 1))
                second_parts(i, (0, 1))
                sqrt_var(i + 1)
                first_parts(i, (2, 3))
                values(i, 0, vps)
                transposed(i + 1, 0)
                second_parts(i, (2, 3))
                values(i, 1, vps)
                transposed(i + 1, 1)
                transposed(i + 1, 2)
            for own in ((0, 1), (2, 3)):
                first_parts(B - 1, own)
                second_parts(B - 1, own)
            for k in range(2):
                values(B - 1, k, vps_last)

            def max_rows(b, slot, par):
                act.wait_ge(s_mt, UNITS * b + slot + 1)
                nc.scalar.activation(m_rows[:, par, :], mt_ps[0:MROWS * G * T, :], ACT.Identity)\
                  .then_inc(s_mtev, 1)

            def unit_output(b, g):
                u = UNITS * b + g
                act.wait_ge(s_pv, T * (u + 1))
                act.wait_ge(s_ow[g % 2], DMA * (2 * b + g // 2))
                nc.scalar.activation(o_sb[:, g % 2, :], pv_ps, ACT.Identity).then_inc(s_oev, 1)

            def tiles(b, own, last=False, first=False):
                for m in own:
                    g, s, q = m // TILES, m % TILES, m // G
                    act.wait_ge(s_st, TILES * UNITS * b + m + 1)
                    if s % G == 0:
                        act.wait_ge(s_pv, QUADS * b + max(q - 3, 0 if first or q else -3))
                    nc.scalar.activation(probs[:, q % 4, s % G, :], st_ps[m % 2], ACT.Exp, scale=SCALE)\
                      .then_inc(s_exp, 1)
                    if s == 3 and not (m == 3 and first):
                        unit_output(b, g - 1) if g else unit_output(b - 1, UNITS - 1)
                    if s == 11 and not (last and g == UNITS - 1):
                        if g:
                            act.wait_ge(s_mrow[g - 1], DMA * (b + 1))
                        else:
                            act.wait_ge(s_mrow[UNITS - 1], DMA * b)
                        max_rows(b, g + 1, (g + 1) % 2)

            nc.scalar.activation(warm[:, :], eps[:, :], ACT.Exp).then_inc(s_warm, 1)
            max_rows(0, 0, 0)
            tiles(0, range(G), first=True)
            with act.Fori(0, B - 1) as b:
                tiles(b, range(G, TILES * UNITS))
                tiles(b + 1, range(G))
            tiles(B - 1, range(G, TILES * UNITS), last=True)
            unit_output(B - 1, UNITS - 1)

        @block.vector
        def _(dve):
            def statistics(b, n):
                head = isinstance(b, int) and b == 0 and n == 0
                dve.wait_ge(s_x01, DMA) if head else dve.wait_ge((s_lx, s_lc)[n], DMA * (b + 1))
                for t in range(T):
                    if head and t == 2:
                        dve.wait_ge(s_lx, DMA)
                    row = (xin, cin)[n][:, bass.ds(b * T + t, 1), :].rearrange("p a d -> p (a d)")
                    last = nc.vector.bn_stats(stats[:, n * T + t, :], row)
                last.then_inc(s_bs, 1)
                wait_alone(dve, "dve", s_bs, 2 * b + n + 1)
                for t in range(T):
                    last = nc.vector.bn_aggr(mv[:, n * T + t, :], stats[:, n * T + t, :])
                last.then_inc(s_mv, 1)

            def inverse_std(own, done):
                y, y2, vy2, corr = (newton[:, k, own] for k in range(4))
                nc.vector.reciprocal(y, std[:, own]).then_inc(s_nw, 1)
                dve.wait_ge(s_nw, done + 1)
                nc.vector.tensor_tensor(y2, y, y, ALU.mult).then_inc(s_nw, 1)
                dve.wait_ge(s_nw, done + 2)
                nc.vector.scalar_tensor_tensor(out=vy2, in0=mv[:, own, 1], scalar=EPS, in1=y2,
                                               op0=ALU.add, op1=ALU.mult).then_inc(s_nw, 1)
                dve.wait_ge(s_nw, done + 3)
                nc.vector.tensor_scalar(corr, vy2, -0.5, 1.5, ALU.mult, ALU.add).then_inc(s_nw, 1)
                dve.wait_ge(s_nw, done + 4)
                nc.vector.tensor_tensor(rstd[:, own], y, corr, ALU.mult).then_inc(s_nw, 1)
                dve.wait_ge(s_nw, done + 5)

            def normalise(b, n):
                if not isinstance(b, int):
                    dve.wait_ge(s_tr, 4 * b - 2 + 2 * n)
                for t in range(T):
                    k = n * T + t
                    row = (xin, cin)[n][:, bass.ds(b * T + t, 1), :].rearrange("p a d -> p (a d)")
                    last = nc.vector.tensor_scalar(xn[:, n, t, :], row, mv[:, k, 0:1], rstd[:, k:k + 1],
                                                   ALU.subtract, ALU.mult)
                last.then_inc(s_xn, 1)

            def rest_of(b, k):
                dve.wait_ge(s_p1, 4 * b + k + 1)
                dve.wait_ge(s_p3, 4 * b + k - 1 if k > 1 else 4 * b)
                nc.vector.tensor_tensor(rest[:, k % 2, :], prj[k], parts[:, k, 0, :], ALU.subtract)\
                  .then_inc(s_rest, 1)

            def max_pair(b, g, k):
                t, h = k // 2, k % 2
                dve.wait_ge(s_mx, 2 * T * (UNITS * b + g) + k + 1)
                nc.vector.tensor_reduce(neg_max[:, g, 2 * h:2 * h + 2, t], mx_ps[h], AX.X, ALU.max,
                                        negate=True).then_inc(s_red, 1)

            nc.vector.memset(eps[:, :], EPS).then_inc(s_eps, 1)
            nc.vector.memset(heat[:, :], 0.0).then_inc(s_heat, 1)
            for n in range(2):
                statistics(0, n)
                dve.wait_ge(s_sd, n + 1)
                inverse_std(bass.ts(n, T), 5 * n)
                normalise(0, n)
            dve.wait_ge(s_cst, 2 * DMA)
            nc.vector.tensor_copy(ident_b[:, :], ident[:, :]).then_inc(s_ib, 1)
            with dve.Fori(0, B - 1) as i:
                for n in range(2):
                    statistics(i + 1, n)
                rest_of(i, 0)
                rest_of(i, 1)
                dve.wait_ge(s_sd, 2 * i + 4)
                inverse_std(slice(0, 2 * T), 5 * i + 10)
                normalise(i + 1, 0)
                rest_of(i, 2)
                rest_of(i, 3)
                normalise(i + 1, 1)
            rest_of(B - 1, 0)
            rest_of(B - 1, 1)
            for k in range(2 * T):
                if k in (4, 6):
                    rest_of(B - 1, 2 + (k - 4) // 2)
                max_pair(0, 0, k)

            def recip(b):
                dve.wait_ge(s_ds, 2 * DMA * UNITS * (b + 1))
                nc.vector.reciprocal(recips[:, b, :], sums[:, b, :]).then_inc(s_rc, 1)

            for g in range(1, UNITS):
                for k in range(2 * T):
                    max_pair(0, g, k)
            with dve.Fori(1, B) as b:
                for g in range(UNITS):
                    dve.wait_ge(s_mp, UNITS * b + g - UNITS + 1)
                    for k in range(2 * T):
                        max_pair(b, g, k)
                    if g == 2:
                        recip(b - 1)
            recip(B - 1)
            with dve.Fori(0, B // 2) as i:
                for par in range(2):
                    for h in range(2):
                        k = 2 * par + h
                        dve.wait_ge(s_fc, 4 * i + k + 1)
                        dve.wait_ge(s_xr, B)
                        dst = xin[:, bass.ds(i * 2 * T + 2 * k, 2)]
                        nc.vector.tensor_tensor(dst, ps[:, k, :].rearrange("p (t n) -> p t n", t=2), dst, ALU.add)\
                          .then_inc(s_fin, 1)

        @block.tensor
        def _(pe):
            def transposes(b, n):
                pe.wait_ge(s_xn, 2 * b + n + 1)
                if not isinstance(b, int):
                    pe.wait_ge(s_tev, 6 * b - (4, 0)[n])
                for f in range(FT):
                    for t in range(T):
                        last = nc.tensor.transpose(trn[FT * n + f][:, bass.ts(t, P)],
                                                   xn[:, n, t, bass.ts(f, P)], ident[:, :])
                    last.then_inc(s_tr, 1)

            def projection_step(k, f):
                r = nc.tensor.matmul(prj[k], w_sb["qk"[k // 2]][:, f, bass.ts(k % 2, P)], lnT[:, k // 2, f, :],
                                     start=(f == 0), stop=(f == FT - 1))
                if f == FT - 1:
                    r.then_inc(s_prj, 1)

            def projections(b, n):
                pe.wait_ge(s_tev, 6 * b + 2 * n + 2)
                for k in (2 * n, 2 * n + 1):
                    if not isinstance(b, int):
                        if n == 0:
                            pe.wait_ge(s_vev, 2 * b - 1 + k)
                        else:
                            pe.wait_ge(s_rest, 4 * b)
                    for f in range(FT):
                        projection_step(k, f)

            def values_step(k, h, bank):
                for f in range(FT):
                    r = nc.tensor.matmul(bank[:, bass.ts(h, DM)], lnT[:, 2, f, bass.ts(2 * k + h, P)],
                                         w_sb["v"][:, f, :], start=(f == 0), stop=(f == FT - 1))
                if h:
                    r.then_inc(s_vprj, 1)

            def values(b, k):
                pe.wait_ge(s_tev, 6 * b + 6)
                pe.wait_ge(s_rest, 4 * b + k + 1)
                for h in range(2):
                    values_step(k, h, vps[k])

            def max_tile(b, n):
                g, t, j = n // TILES, n % TILES // G, n % G
                b, g = b + g // UNITS, g % UNITS
                if n % TILES == 0:
                    pe.wait_ge(s_load[g], 2 * DMA * (b + 1))
                if j % 2 == 0 and not (isinstance(b, int) and b == 0 and n < 4):
                    pe.wait_ge(s_red, (TILES * UNITS * b + n % (TILES * UNITS)) // 2 - 1 if isinstance(b, int)
                               else TILES * UNITS // 2 * b + n % (TILES * UNITS) // 2 - 1)
                r = nc.tensor.matmul(mx_ps[j // 2][:, j % 2, :], qs[0:ROWS, g, j, bass.ts(t, P)], ks[0:ROWS, g, j, :],
                                     start=True, stop=True)
                if j % 2:
                    r.then_inc(s_mx, 1)

            def max_transpose(b, slot, par):
                w = UNITS * b + slot
                pe.wait_ge(s_mp, w + 1)
                wait_alone(pe, "pe", s_mtev, w)
                nc.tensor.transpose(mt_ps[0:MROWS * G * T, :], m_parts[:, par].rearrange("p c n -> p (c n)"),
                                    ident_b[:, :]).then_inc(s_mt, 1)

            def score_tile(b, m):
                g, t, j = m // TILES, m % TILES // G, m % G
                if m % TILES == 0:
                    pe.wait_ge(s_mrow[g], DMA * (b + 1))
                if m > 1:
                    pe.wait_ge(s_exp, TILES * UNITS * b + m - 1)
                elif m == 0:
                    pe.wait_ge(s_exp, TILES * UNITS * b)
                nc.tensor.matmul(st_ps[m % 2], ks[0:ROWS + MROWS, g, j, bass.ts(t, P)], qs[0:ROWS + MROWS, g, j, :],
                                 start=True, stop=True).then_inc(s_st, 1)

            def values_product(b, q, half):
                g, t = q // T, q % T
                u = UNITS * b + g
                if half == 0:
                    if t == 0:
                        pe.wait_ge(s_vst, u + 1)
                        pe.wait_ge(s_oev, u)
                    pe.wait_ge(s_exp, TILES * UNITS * b + G * (q + 1))
                own = bass.ts(half, S // 2)
                for j in range(G):
                    last = nc.tensor.matmul(pv_ps[32 * j:32 * j + 32, own], v_st[:, g, t, j, :],
                                            probs[:, q % 4, j, own], start=(t == 0 and half == 0),
                                            stop=(t == T - 1 and half == 1), skip_group_check=True)
                if half:
                    last.then_inc(s_pv, 1)

            def quad(b, q, last=False, first=False):
                score, bound = G * q, TILES * UNITS if last else 2 * TILES * UNITS
                for half in range(2):
                    for j in (2 * half, 2 * half + 1):
                        score_tile(b, score + j)
                        if score + j + LEAD < bound:
                            max_tile(b, score + j + LEAD)
                    if half and q % T == T - 2 and not (last and q > QUADS - T):
                        max_transpose(b, q // T + 1, (q // T + 1) % 2)
                    if q:
                        values_product(b, q - 1, half)
                    elif not first:
                        values_product(b - 1, QUADS - 1, half)

            pe.wait_ge(s_heat, 1)
            for k in range(16):
                nc.tensor.matmul(ps[:, 7], heat[:, 0:P], heat[:, :], start=True, stop=True)
            pe.wait_ge(s_cst, 2 * DMA)
            transposes(0, 0)
            for k in range(4):
                nc.tensor.matmul(ps[:, 7], heat[:, 0:P], heat[:, :], start=True, stop=True)
            pe.wait_ge(s_wq, DMA)
            projections(0, 0)
            transposes(0, 1)
            pe.wait_ge(s_w, 4 * DMA)
            with pe.Fori(0, B - 1) as i:
                projections(i, 1)
                values(i, 0)
                transposes(i + 1, 0)
                values(i, 1)
                transposes(i + 1, 1)
                projections(i + 1, 0)

            done = B - 1
            steps = [("k", k, f) for k in (2, 3) for f in range(FT)] + [("v", k, h) for k in range(2) for h in range(2)]
            pe.wait_ge(s_ones, 1)
            pe.wait_ge(s_tev, 6 * done + 6)
            for n in range(LEAD):
                if n == 2:
                    pe.wait_ge(s_rest, 4 * done + 2)
                if n == TILES + 4:
                    pe.wait_ge(s_ib, 1)
                    max_transpose(0, 0, 0)
                max_tile(0, n)
                if n % 2 and n > 2 and steps:
                    kind, k, part = steps.pop(0)
                    if kind == "k":
                        projection_step(k, part)
                    else:
                        values_step(k, part, vps_last[k])
            pe.wait_ge(s_rest, 4 * B)
            pe.wait_ge(s_vev, 2 * B)
            pe.wait_ge(s_vones, 1)
            quad(0, 0, first=True)
            with pe.Fori(0, B - 1) as b:
                for q in range(1, QUADS):
                    quad(b, q)
                quad(b + 1, 0)
            for q in range(1, QUADS):
                quad(B - 1, q, last=True)
            for half in range(2):
                values_product(B - 1, QUADS - 1, half)

            pe.wait_ge(s_oev, B * UNITS)
            with pe.Fori(0, B // 2) as i:
                for par in range(2):
                    pe.wait_ge(s_ct, 4 * i + 2 * par + 2)
                    if par == 0:
                        pe.wait_ge(s_fin, 4 * i)
                    for t in range(T):
                        for half in range(2):
                            last = nc.tensor.matmul(ps[:, 2 * par + t // 2, bass.ts(t % 2, DM)],
                                                    ctxT[:, par, half, bass.ts(t, P)], w_sb["fc"][:, half, :],
                                                    start=(half == 0), stop=(half == 1))
                        if t % 2:
                            last.then_inc(s_fc, 1)


def kernel(x, ctx_1024, L0_xattn_ln_q_g, L0_xattn_ln_q_b, L0_xattn_ln_k_g, L0_xattn_ln_k_b, L0_xattn_ln_v_g,
           L0_xattn_ln_v_b, L0_xattn_w_q, L0_xattn_w_k, L0_xattn_w_v, L0_xattn_w_fc, L0_xattn_b_fc):
    import numpy as np
    import concourse.bacc as bacc
    from concourse.bass_utils import run_bass_kernel_spmd

    def by_dimension(w):
        return np.ascontiguousarray(np.asarray(w).T.reshape(DM, 2, HEADS // 2, HD).transpose(0, 1, 3, 2)
                                    .reshape(DM, DM))

    vectors = (L0_xattn_ln_q_g, L0_xattn_ln_q_b, L0_xattn_ln_k_g, L0_xattn_ln_k_b, L0_xattn_ln_v_g, L0_xattn_ln_v_b)
    arrays = {
        "x": np.asarray(x),
        "context": np.asarray(ctx_1024),
        "wqT": by_dimension(L0_xattn_w_q),
        "wkT": by_dimension(L0_xattn_w_k),
        "wvT": np.ascontiguousarray(np.asarray(L0_xattn_w_v).T),
        "wfcT": np.ascontiguousarray(np.asarray(L0_xattn_w_fc).T),
        "ln_cols": np.ascontiguousarray(np.stack([np.asarray(v).reshape(FT, P) for v in vectors]).transpose(2, 0, 1)),
        "b_fc": np.asarray(L0_xattn_b_fc),
        "eye": np.eye(P, dtype=np.float32),
    }
    nc = bacc.Bacc("TRN2", target_bir_lowering=False, num_devices=1)
    args = [nc.dram_tensor(n, a.shape, mybir.dt.from_np(a.dtype), kind="ExternalInput").ap()
            for n, a in arrays.items()]
    out = nc.dram_tensor("out", (B, S, DM), F32, kind="ExternalOutput").ap()
    build(nc, *args, out)
    result = run_bass_kernel_spmd(nc, [arrays], core_ids=[0])
    return result.results[0]["out"]
```

```python
from contextlib import ExitStack

import concourse.bass as bass
from concourse import mybir

F32 = mybir.dt.float32
BF16 = mybir.dt.bfloat16
ALU = mybir.AluOpType
ACT = mybir.ActivationFunctionType
AX = mybir.AxisListType

P = 128
B, S, DM = 4, 512, 256
HEADS, HD = 16, 16
G = 4
UNITS = HEADS // G
T = S // P
FT = DM // P
ROWS = 6 * HD
MROWS = 3
TILES = T * G
QUADS = T * UNITS
TAIL = TILES * UNITS - 24
LEAD = 26
EPS = 1e-5
SCALE = float(HD) ** -0.5
QPARTS = ((0, 0, 3), (3, 1, 2), (5, 2, 1))
EARLY_OUT = {(11, 1): (0, 0), (13, 0): (0, 1), (QUADS, 0): (0, 2)}
EARLY_PAIRS = 2
DMA = 16


def build(nc, x, ctx_in, wq, wk, wv, wfc, ln_cols, b_fc, eye, out):
    with ExitStack() as stack:
        def sb(name, shape, dt=F32):
            return stack.enter_context(nc.sbuf_tensor(name, shape, dt))

        def sem(name):
            return stack.enter_context(nc.semaphore(name))

        q_rows = nc.dram_tensor("q_rows", (B, 2, 6, HD, HEADS // 2, S), BF16, kind="Internal").ap()
        k_rows = nc.dram_tensor("k_rows", (B, 2, 6, HD, HEADS // 2, S), BF16, kind="Internal").ap()
        unit_out = nc.dram_tensor("unit_out", (B, UNITS, G, 32, S), F32, kind="Internal").ap()
        recip_rows = nc.dram_tensor("recip_rows", (B - 1, HEADS, S), F32, kind="Internal").ap()

        ident = sb("ident", [P, P])
        ident_b = sb("ident_b", [P, P], BF16)
        w_sb = {n: sb("w_" + n, [P, FT, DM]) for n in ("q", "k", "v", "fc")}
        lnc = sb("lnc", [P, 6, FT])
        bias = sb("bias", [P, DM])
        eps = sb("eps", [P, 1])
        warm = sb("warm", [P, 1])
        heat = sb("heat", [P, S], BF16)
        xin = sb("xin", [P, B * T, DM])
        cin = sb("cin", [P, B * T, DM])
        xn = sb("xn", [P, 2, T, DM])
        stats = sb("stats", [P, 2 * T, 6])
        mv = sb("mv", [P, 2 * T, 2])
        std = sb("std", [P, 2 * T])
        newton = sb("newton", [P, 4, 2 * T])
        rstd = sb("rstd", [P, 2 * T])
        lnT = sb("lnT", [P, 3, FT, S])
        parts = sb("parts", [P, 4, 3, S], BF16)
        rest = sb("rest", [P, 2, S])
        v_all = sb("v_all", [P, B * T, DM])
        qs = sb("qs", [P, UNITS, G, S], BF16)
        ks = sb("ks", [P, UNITS, G, S], BF16)
        neg_max = sb("neg_max", [P, 4, G, T])
        m_rest = sb("m_rest", [P, 2, G * T])
        m_parts = sb("m_parts", [P, 2, MROWS, G * T], BF16)
        m_rows = sb("m_rows", [MROWS * G * T, 2, P], BF16)
        v_st = sb("v_st", [P, UNITS, T, G, 32])
        zeros = sb("zeros", [P, T * G * HD])
        probs = sb("probs", [P, 4, G, S])
        o_sb = sb("o_sb", [P, 2, S])
        heads_out = cin[:, :, :].rearrange("p a b -> p (a b)").rearrange("p (h t) -> p h t", h=2)
        sums = sb("sums", [P, B - 1, S // 8])
        recips = sb("recips", [P, B - 1, S // 8])
        r_all = sb("r_all", [P, 2, B * S])
        ctxT = sb("ctxT", [P, 2, 2, S])

        ps = stack.enter_context(nc.psum_tensor("ps", [P, 8, S], F32))
        trn = [ps[:, k] for k in (0, 1, 2, 3)]
        prj = [ps[:, k] for k in (4, 5, 6, 7)]
        vps, vps_last = [ps[:, k] for k in (4, 5)], [ps[:, k] for k in (0, 6)]
        st_ps = [ps[:, k] for k in range(4)]
        mx_ps = [ps[:, 2 + 2 * k:4 + 2 * k] for k in range(2)]
        early_mx = ps[:, 6:8]
        pv_ps = ps[:, 6]
        fc_ps = [[ps[:, k, 0:DM] for k in own] for own in ((4, 5, 7, 0), (1, 2, 3, 6))]
        mt_ps = ps[:, 7, 0:P // 2].bitcast(BF16)

        s_x01, s_lx, s_lc, s_cst, s_wq, s_w = (sem("s_x01"), sem("s_lx"), sem("s_lc"), sem("s_cst"), sem("s_wq"),
                                               sem("s_w"))
        s_ib, s_eps = sem("s_ib"), sem("s_eps")
        s_bs, s_mv, s_sd, s_nw, s_xn = sem("s_bs"), sem("s_mv"), sem("s_sd"), sem("s_nw"), sem("s_xn")
        s_tr, s_tev, s_prj, s_vprj, s_vev = sem("s_tr"), sem("s_tev"), sem("s_prj"), sem("s_vprj"), sem("s_vev")
        s_p1, s_rest, s_p2, s_p3, s_xr = sem("s_p1"), sem("s_rest"), sem("s_p2"), sem("s_p3"), sem("s_xr")
        s_pw = [sem(f"s_pw{k}") for k in range(4)]
        s_load = [sem(f"s_load{g}") for g in range(UNITS)]
        s_mrow = [sem(f"s_mrow{g}") for g in range(UNITS)]
        s_ones, s_vones = sem("s_ones"), sem("s_vones")
        s_mx, s_red, s_mstep, s_mp, s_mt, s_mtev = (sem("s_mx"), sem("s_red"), sem("s_mstep"), sem("s_mp"),
                                                    sem("s_mt"), sem("s_mtev"))
        s_st, s_exp, s_vst, s_pv, s_oev = sem("s_st"), sem("s_exp"), sem("s_vst"), sem("s_pv"), sem("s_oev")
        s_ow = [sem(f"s_ow{k}") for k in range(2)]
        s_dh, s_ds, s_rc, s_rw, s_rr = sem("s_dh"), sem("s_ds"), sem("s_rc"), sem("s_rw"), sem("s_rr")
        s_ct, s_fc, s_fin, s_out = sem("s_ct"), sem("s_fc"), sem("s_fin"), sem("s_out")

        x_t = x.rearrange("b (t p) d -> b p t d", p=P)
        c_t = ctx_in.rearrange("b (t p) d -> b p t d", p=P)
        out_t = out.rearrange("b (t p) d -> b p t d", p=P)

        def is_zero(b):
            return isinstance(b, int) and b == 0

        def score_bank(m, last):
            if last and m >= TAIL:
                return st_ps[m % 4], (2 if m < TAIL + 2 else 4)
            return st_ps[m % 2], 2

        s_zero, s_warm, s_heat = sem("s_zero"), sem("s_warm"), sem("s_heat")
        s_own = {e: sem("s_own_" + e) for e in ("sp", "dve", "pe")}

        def wait_alone(eng, name, semaphore, value):
            eng.wait_ge(semaphore, value)
            eng.sem_inc(s_own[name], 1)

        block = stack.enter_context(nc.Block())

        @block.sync
        def _(sp):
            def load_inputs(b):
                sp.dma_start(xin[:, bass.ts(b, T)], x_t[b]).then_inc(s_lx, DMA)
                sp.dma_start(cin[:, bass.ts(b, T)], c_t[b]).then_inc(s_lc, DMA)

            def write_parts(b, own=range(4)):
                for k in own:
                    wait_alone(sp, "sp", s_p3, 4 * b + k + 1)
                    if k < 2:
                        for row, part, n in QPARTS:
                            dst = q_rows[b, k % 2, row:row + n].rearrange("c d h t -> (d h) c t")
                            src = parts[:, k, part, :].unsqueeze(1).to_broadcast([P, n, S])
                            sp.dma_start(dst, src).then_inc(s_pw[k], DMA)
                    else:
                        for row, n in ((0, 3), (3, 2), (5, 1)):
                            dst = k_rows[b, k % 2, row:row + n].rearrange("c d h t -> (d h) c t")
                            sp.dma_start(dst, parts[:, k, 0:n, :]).then_inc(s_pw[k], DMA)

            def load_stacks(b, g):
                wait_alone(sp, "sp", s_pw[g // 2], 3 * DMA * (b + 1))
                wait_alone(sp, "sp", s_pw[2 + g // 2], 3 * DMA * (b + 1))
                for rows, dst in ((q_rows, qs), (k_rows, ks)):
                    src = rows[b, g // 2, :, :, bass.ts(g % 2, G)].rearrange("c d h t -> (c d) h t")
                    sp.dma_start(dst[0:ROWS, g], src).then_inc(s_load[g], DMA)

            def write_max_rows(w, slot, par):
                wait_alone(sp, "sp", s_mtev, w + 1)
                sp.dma_start(qs[ROWS:ROWS + MROWS, slot], m_rows[:, par, :]).then_inc(s_mrow[slot], DMA)

            def store_unit(b, g):
                u = UNITS * b + g
                wait_alone(sp, "sp", s_oev, u + 1)
                sp.dma_start(unit_out[b, g].rearrange("j r t -> (j r) t"), o_sb[:, g % 2, :])\
                  .then_inc(s_ow[g % 2], DMA)

            def fetch_unit(b, g, last=False):
                u = UNITS * b + g
                wait_alone(sp, "sp", s_ow[g % 2], DMA * (2 * b + g // 2 + 1))
                wait_alone(sp, "sp", s_dh, DMA * u)
                wait_alone(sp, "sp", s_ds, DMA * u)
                rows = 64 * (g % 2)
                if last:
                    sp.dma_start(r_all[rows:rows + 64, g // 2, bass.ts(b, S)],
                                 unit_out[b, g, :, HD:32, :].rearrange("j r t -> r j t")).then_inc(s_ds, DMA)
                else:
                    sp.dma_start(sums[32 * g:32 * g + 32, b, :],
                                 unit_out[b, g, :, HD, :].rearrange("j (c w) -> j c w", c=8)).then_inc(s_ds, DMA)
                sp.dma_start(heads_out[rows:rows + 64, g // 2, bass.ts(b, S)],
                             unit_out[b, g, :, 0:HD, :].rearrange("j r t -> r j t"))\
                  .then_inc(s_dh, DMA)

            def write_recips(b):
                wait_alone(sp, "sp", s_rc, b + 1)
                sp.dma_start(recip_rows[b].rearrange("h (c w) -> (h c) w", c=8), recips[:, b, :])\
                  .then_inc(s_rw, DMA)

            def spread_recips(b):
                wait_alone(sp, "sp", s_rw, DMA * (b + 1))
                wait_alone(sp, "sp", s_rr, UNITS * DMA * b)
                for g in range(UNITS):
                    rows = 64 * (g % 2)
                    src = recip_rows[b, bass.ts(g, G), :].unsqueeze(0).to_broadcast([HD, G, S])
                    sp.dma_start(r_all[rows:rows + 64, g // 2, bass.ts(b, S)], src).then_inc(s_rr, DMA)

            def batch(b, first=False, last=False):
                for g in range(UNITS):
                    if g and not last:
                        wait_alone(sp, "sp", s_st, TILES * (UNITS * b + g))
                        load_stacks(b + 1, g - 1)
                    if g:
                        store_unit(b, g - 1)
                    elif not first:
                        store_unit(b - 1, UNITS - 1)
                    if not (last and g == UNITS - 1):
                        write_max_rows(UNITS * b + g + 1, (g + 1) % UNITS, (g + 1) % 2)
                    if g:
                        fetch_unit(b, g - 1, last)
                    elif not first:
                        fetch_unit(b - 1, UNITS - 1)
                    if g >= 2 and not first:
                        write_recips(b - 1) if g == 2 else spread_recips(b - 1)
                if not last:
                    wait_alone(sp, "sp", s_st, TILES * UNITS * (b + 1))
                    load_stacks(b + 1, UNITS - 1)

            sp.dma_start(xin[:, 0:2], x_t[0][:, 0:2]).then_inc(s_x01, DMA)
            sp.dma_start(xin[:, 2:T], x_t[0][:, 2:T]).then_inc(s_lx, DMA)
            sp.dma_start(ident[:, :], eye).then_inc(s_cst, DMA)
            sp.dma_start(lnc[:, :, :], ln_cols).then_inc(s_cst, DMA)
            sp.dma_start(w_sb["q"][:, :, :], wq.rearrange("(f p) n -> p f n", p=P)).then_inc(s_wq, DMA)
            sp.dma_start(cin[:, 0:T], c_t[0]).then_inc(s_lc, DMA)
            for n, w in (("k", wk), ("v", wv), ("fc", wfc)):
                sp.dma_start(w_sb[n][:, :, :], w.rearrange("(f p) n -> p f n", p=P)).then_inc(s_w, DMA)
            sp.dma_start(bias[:, :], b_fc.partition_broadcast(P)).then_inc(s_w, DMA)
            with sp.Fori(1, B) as i:
                wait_alone(sp, "sp", s_lx, DMA * i)
                wait_alone(sp, "sp", s_lc, DMA * i)
                load_inputs(i)
            write_parts(0)
            load_stacks(0, 0)
            load_stacks(0, 1)
            with sp.Fori(1, B - 1) as i:
                write_parts(i)
            load_stacks(0, 2)
            write_parts(B - 1, (0, 1))
            write_max_rows(0, 0, 0)
            write_parts(B - 1, (2, 3))
            load_stacks(0, 3)
            batch(0, first=True)
            with sp.Fori(1, B - 1) as b:
                batch(b)
            batch(B - 1, last=True)
            store_unit(B - 1, UNITS - 1)
            fetch_unit(B - 1, UNITS - 1, last=True)
            with sp.Fori(0, B - 1) as b:
                for h in range(2):
                    wait_alone(sp, "sp", s_fin, T * b + 2 * h + 2)
                    sp.dma_start(out_t[b][:, bass.ts(h, 2)], xin[:, bass.ds(b * T + 2 * h, 2)])\
                      .then_inc(s_out, DMA)
            for first, n in ((0, 2), (2, 1), (3, 1)):
                wait_alone(sp, "sp", s_fin, T * (B - 1) + first + n)
                sp.dma_start(out_t[B - 1][:, first:first + n], xin[:, bass.ds((B - 1) * T + first, n)])\
                  .then_inc(s_out, DMA)
            wait_alone(sp, "sp", s_out, DMA * (2 * B + 1))

        @block.gpsimd
        def _(pool):
            nc.gpsimd.memset(ks[ROWS:P, :, :, :], 1.0).then_inc(s_ones, 1)
            pool.wait_ge(s_ones, 1)
            nc.gpsimd.memset(v_st[:, :, :, :, HD:32], 1.0).then_inc(s_vones, 1)
            nc.gpsimd.memset(zeros[:, :], 0.0).then_inc(s_zero, 1)
            pool.wait_ge(s_zero, 1)
            pool.wait_ge(s_w, 4 * DMA)

            def third_parts(b, own):
                for k in own:
                    pool.wait_ge(s_p2, 4 * b + k + 1)
                    nc.gpsimd.tensor_tensor(parts[:, k, 2, :], rest[:, k % 2, :], parts[:, k, 1, :],
                                            ALU.subtract).then_inc(s_p3, 1)

            def add_bias(b):
                pool.wait_ge(s_xn, 4 * b + 2)
                nc.gpsimd.tensor_tensor(xin[:, bass.ts(b, T)], xin[:, bass.ts(b, T)],
                                        bias[:, :].unsqueeze(1).to_broadcast([P, T, DM]), ALU.add)\
                  .then_inc(s_xr, 1)

            def minus_max_parts(b, g, first=False):
                w = UNITS * b + g
                pool.wait_ge(s_red, 2 * T * (w + 1))
                if not (first and g < 2):
                    pool.wait_ge(s_mt, w - 1)
                src = neg_max[:, g, :, :].rearrange("p j t -> p (j t)")
                mp, mr = m_parts[:, g % 2], m_rest[:, :, :]
                nc.gpsimd.tensor_tensor(mp[:, 0, :], src, zeros[:, 0:G * T], ALU.add).then_inc(s_mstep, 1)
                pool.wait_ge(s_mstep, 4 * w + 1)
                nc.gpsimd.tensor_tensor(mr[:, 0, :], src, mp[:, 0, :], ALU.subtract).then_inc(s_mstep, 1)
                pool.wait_ge(s_mstep, 4 * w + 2)
                nc.gpsimd.tensor_tensor(mp[:, 1, :], mr[:, 0, :], zeros[:, 0:G * T], ALU.add).then_inc(s_mstep, 1)
                pool.wait_ge(s_mstep, 4 * w + 3)
                nc.gpsimd.tensor_tensor(mp[:, 2, :], mr[:, 0, :], mp[:, 1, :], ALU.subtract).then_inc(s_mstep, 1)
                pool.wait_ge(s_mstep, 4 * w + 4)
                pool.sem_inc(s_mp, 1)

            def stage_values(b, g, first=False):
                w = UNITS * b + g
                if not first:
                    pool.wait_ge(s_pv, T * (w - UNITS + 1))
                nc.gpsimd.tensor_tensor(
                    v_st[:, g, :, :, 0:HD],
                    v_all[:, bass.ts(b, T), G * HD * g:G * HD * (g + 1)].rearrange("p t (j d) -> p t j d", j=G),
                    zeros[:, :].rearrange("p (t j d) -> p t j d", t=T, j=G), ALU.add).then_inc(s_vst, 1)

            def divide(b):
                pool.wait_ge(s_dh, DMA * (UNITS * b + 2))
                if b >= 2:
                    pool.wait_ge(s_fc, T * (b - 1))
                if b < B - 1:
                    pool.wait_ge(s_rr, UNITS * DMA * (b + 1))
                else:
                    pool.wait_ge(s_rc, B)
                nc.gpsimd.tensor_tensor(ctxT[:, b % 2, 0, :], heads_out[:, 0, bass.ts(b, S)],
                                        r_all[:, 0, bass.ts(b, S)], ALU.mult).then_inc(s_ct, 1)
                pool.wait_ge(s_dh, DMA * UNITS * (b + 1))
                for t in range(T):
                    if b == B - 1:
                        pool.wait_ge(s_rc, B + 1 + t)
                    nc.gpsimd.tensor_tensor(ctxT[:, b % 2, 1, bass.ts(t, P)], heads_out[:, 1, bass.ts(b * T + t, P)],
                                            r_all[:, 1, bass.ts(b * T + t, P)], ALU.mult).then_inc(s_ct, 1)

            with pool.Fori(0, B - 1) as i:
                third_parts(i, range(4))
                add_bias(i)
            third_parts(B - 1, (0, 1))
            minus_max_parts(0, 0, first=True)
            third_parts(B - 1, (2, 3))
            pool.wait_ge(s_vev, 2 * (B - 1))
            stage_values(0, 0, first=True)
            add_bias(B - 1)
            for g in range(1, UNITS):
                minus_max_parts(0, g, first=True)
                stage_values(0, g, first=True)
            pool.wait_ge(s_vev, 2 * B)
            with pool.Fori(1, B - 1) as b:
                for g in range(UNITS):
                    minus_max_parts(b, g)
                    stage_values(b, g)
            for g in range(UNITS):
                minus_max_parts(B - 1, g)
                stage_values(B - 1, g)
                if g < 2:
                    divide(g)
            divide(2)
            divide(3)

        @block.scalar
        def _(act):
            def sqrt_var(b, which=(0, 1)):
                for n in which:
                    act.wait_ge(s_mv, 2 * b + n + 1)
                    nc.scalar.activation(std[:, bass.ts(n, T)], mv[:, bass.ts(n, T), 1], ACT.Sqrt,
                                         bias=eps[:, 0:1]).then_inc(s_sd, 1)

            def transposed(b, n):
                for f in range(FT):
                    k = FT * min(n, 1) + f
                    act.wait_ge(s_tr, 4 * b + k + 1)
                    nc.scalar.activation(lnT[:, n, f, :], trn[k], ACT.Identity,
                                         scale=lnc[:, 2 * n, f:f + 1], bias=lnc[:, 2 * n + 1, f:f + 1])\
                      .then_inc(s_tev, 1)

            def first_parts(b, own):
                for k in own:
                    act.wait_ge(s_prj, 4 * b + k + 1)
                    act.wait_ge(s_pw[k], 3 * DMA * b)
                    nc.scalar.activation(parts[:, k, 0, :], prj[k], ACT.Identity).then_inc(s_p1, 1)

            def second_parts(b, own):
                for k in own:
                    act.wait_ge(s_rest, 4 * b + k + 1)
                    nc.scalar.activation(parts[:, k, 1, :], rest[:, k % 2, :], ACT.Identity).then_inc(s_p2, 1)

            def values(b, k, vps):
                act.wait_ge(s_vprj, 2 * b + k + 1)
                nc.scalar.activation(v_all[:, bass.ds(b * T + 2 * k, 2)],
                                     vps[k].rearrange("p (t n) -> p t n", t=2), ACT.Identity)\
                  .then_inc(s_vev, 1)

            act.wait_ge(s_eps, 1)
            nc.scalar.activation(warm[:, :], eps[:, :], ACT.Sqrt).then_inc(s_warm, 1)
            sqrt_var(0, (0,))
            act.wait_ge(s_cst, 2 * DMA)
            transposed(0, 0)
            sqrt_var(0, (1,))
            first_parts(0, (0,))
            transposed(0, 1)
            transposed(0, 2)
            first_parts(0, (1,))
            with act.Fori(0, B - 1) as i:
                second_parts(i, (0, 1))
                sqrt_var(i + 1)
                first_parts(i, (2, 3))
                values(i, 0, vps)
                transposed(i + 1, 0)
                second_parts(i, (2, 3))
                values(i, 1, vps)
                transposed(i + 1, 1)
                transposed(i + 1, 2)
                first_parts(i + 1, (0, 1))
            second_parts(B - 1, (0, 1))
            nc.scalar.activation(warm[:, :], eps[:, :], ACT.Exp).then_inc(s_warm, 1)
            first_parts(B - 1, (2, 3))
            values(B - 1, 0, vps_last)

            def max_rows(b, slot, par):
                act.wait_ge(s_mt, UNITS * b + slot + 1)
                nc.scalar.activation(m_rows[:, par, :], mt_ps[0:MROWS * G * T, :], ACT.Identity)\
                  .then_inc(s_mtev, 1)

            def unit_output(b, g):
                u = UNITS * b + g
                act.wait_ge(s_pv, T * (u + 1))
                act.wait_ge(s_ow[g % 2], DMA * (2 * b + g // 2))
                nc.scalar.activation(o_sb[:, g % 2, :], pv_ps, ACT.Identity).then_inc(s_oev, 1)

            def tiles(b, own, last=False, first=False):
                for m in own:
                    g, s, q = m // TILES, m % TILES, m // G
                    act.wait_ge(s_st, TILES * UNITS * b + m + 1)
                    if s % G == 0:
                        act.wait_ge(s_pv, QUADS * b + max(q - 3, 0 if first or q else -3))
                    nc.scalar.activation(probs[:, q % 4, s % G, :], score_bank(m, last)[0], ACT.Exp, scale=SCALE)\
                      .then_inc(s_exp, 1)
                    if s == 3 and not (m == 3 and first):
                        unit_output(b, g - 1) if g else unit_output(b - 1, UNITS - 1)
                    if s == 9 and not (last and g == UNITS - 1):
                        if g:
                            act.wait_ge(s_mrow[g - 1], DMA * (b + 1))
                        else:
                            act.wait_ge(s_mrow[UNITS - 1], DMA * b)
                        max_rows(b, g + 1, (g + 1) % 2)

            max_rows(0, 0, 0)
            second_parts(B - 1, (2, 3))
            values(B - 1, 1, vps_last)
            tiles(0, range(G), first=True)
            with act.Fori(0, B - 1) as b:
                tiles(b, range(G, TILES * UNITS))
                tiles(b + 1, range(G))
            tiles(B - 1, range(G, TILES * UNITS), last=True)
            unit_output(B - 1, UNITS - 1)

        @block.vector
        def _(dve):
            def statistics(b, n):
                head = is_zero(b) and n == 0
                dve.wait_ge(s_x01, DMA) if head else dve.wait_ge((s_lx, s_lc)[n], DMA * (b + 1))
                for t in range(T):
                    if head and t == 2:
                        dve.wait_ge(s_lx, DMA)
                    row = (xin, cin)[n][:, bass.ds(b * T + t, 1), :].rearrange("p a d -> p (a d)")
                    last = nc.vector.bn_stats(stats[:, n * T + t, :], row)
                last.then_inc(s_bs, 1)
                wait_alone(dve, "dve", s_bs, 2 * b + n + 1)
                for t in range(T):
                    last = nc.vector.bn_aggr(mv[:, n * T + t, :], stats[:, n * T + t, :])
                last.then_inc(s_mv, 1)

            def inverse_std(own, done):
                y, y2, vy2, corr = (newton[:, k, own] for k in range(4))
                nc.vector.reciprocal(y, std[:, own]).then_inc(s_nw, 1)
                dve.wait_ge(s_nw, done + 1)
                nc.vector.tensor_tensor(y2, y, y, ALU.mult).then_inc(s_nw, 1)
                dve.wait_ge(s_nw, done + 2)
                nc.vector.scalar_tensor_tensor(out=vy2, in0=mv[:, own, 1], scalar=EPS, in1=y2,
                                               op0=ALU.add, op1=ALU.mult).then_inc(s_nw, 1)
                dve.wait_ge(s_nw, done + 3)
                nc.vector.tensor_scalar(corr, vy2, -0.5, 1.5, ALU.mult, ALU.add).then_inc(s_nw, 1)
                dve.wait_ge(s_nw, done + 4)
                nc.vector.tensor_tensor(rstd[:, own], y, corr, ALU.mult).then_inc(s_nw, 1)
                dve.wait_ge(s_nw, done + 5)

            def normalise(b, n):
                if not is_zero(b):
                    dve.wait_ge(s_tr, 4 * b - 2 + 2 * n)
                for t in range(T):
                    k = n * T + t
                    row = (xin, cin)[n][:, bass.ds(b * T + t, 1), :].rearrange("p a d -> p (a d)")
                    r = nc.vector.tensor_scalar(xn[:, n, t, :], row, mv[:, k, 0:1], rstd[:, k:k + 1],
                                                ALU.subtract, ALU.mult)
                    if t % 2:
                        r.then_inc(s_xn, 1)

            def rest_of(b, k):
                dve.wait_ge(s_p1, 4 * b + k + 1)
                dve.wait_ge(s_p3, 4 * b + k - 1 if k > 1 else 4 * b)
                nc.vector.tensor_tensor(rest[:, k % 2, :], prj[k], parts[:, k, 0, :], ALU.subtract)\
                  .then_inc(s_rest, 1)

            def max_pair(b, g, k, bank=None):
                t, h = k // 2, k % 2
                dve.wait_ge(s_mx, 2 * T * (UNITS * b + g) + k + 1)
                scores = mx_ps[h] if bank is None else bank
                nc.vector.tensor_reduce(neg_max[:, g, 2 * h:2 * h + 2, t], scores, AX.X, ALU.max,
                                        negate=True).then_inc(s_red, 1)

            nc.vector.memset(eps[:, :], EPS).then_inc(s_eps, 1)
            nc.vector.memset(heat[:, :], 0.0).then_inc(s_heat, 1)
            for n in range(2):
                statistics(0, n)
                dve.wait_ge(s_sd, n + 1)
                inverse_std(bass.ts(n, T), 5 * n)
                normalise(0, n)
            dve.wait_ge(s_cst, 2 * DMA)
            nc.vector.tensor_copy(ident_b[:, :], ident[:, :]).then_inc(s_ib, 1)

            def phase1(i, early_pairs=0):
                for n in range(2):
                    statistics(i + 1, n)
                rest_of(i, 0)
                rest_of(i, 1)
                dve.wait_ge(s_sd, 2 * i + 4)
                inverse_std(slice(0, 2 * T), 5 * i + 10)
                normalise(i + 1, 0)
                rest_of(i, 2)
                rest_of(i, 3)
                normalise(i + 1, 1)
                for k in range(early_pairs):
                    max_pair(0, 0, k, early_mx)

            with dve.Fori(0, B - 2) as i:
                phase1(i)
            phase1(B - 2, EARLY_PAIRS)
            rest_of(B - 1, 0)
            rest_of(B - 1, 1)
            for k in range(EARLY_PAIRS, 2 * T):
                max_pair(0, 0, k)
            rest_of(B - 1, 2)
            rest_of(B - 1, 3)

            def recip(b):
                dve.wait_ge(s_ds, DMA * UNITS * (b + 1))
                nc.vector.reciprocal(recips[:, b, :], sums[:, b, :]).then_inc(s_rc, 1)

            for g in range(1, UNITS):
                for k in range(2 * T):
                    max_pair(0, g, k)
            with dve.Fori(1, B) as b:
                for g in range(UNITS):
                    dve.wait_ge(s_mp, UNITS * b + g - UNITS + 1)
                    for k in range(2 * T):
                        max_pair(b, g, k)
                    if g == 2:
                        recip(b - 1)

            def recip_rows_of(half, own):
                dve.wait_ge(s_ds, DMA * (UNITS * (B - 1) + 2 * half + 2))
                nc.vector.reciprocal(r_all[:, half, own], r_all[:, half, own]).then_inc(s_rc, 1)

            def add_input(b, tiles=range(T)):
                dve.wait_ge(s_xr, b + 1)
                for t in tiles:
                    dve.wait_ge(s_fc, T * b + t + 1)
                    dst = xin[:, b * T + t, :]
                    nc.vector.tensor_tensor(dst, fc_ps[b % 2][t], dst, ALU.add)\
                      .then_inc(s_fin, 1)

            recip_rows_of(0, bass.ts(B - 1, S))
            for b in range(B - 2):
                add_input(b)
            add_input(B - 2, (0, 1))
            for t in range(T):
                recip_rows_of(1, bass.ts((B - 1) * T + t, P))
            add_input(B - 2, (2, 3))
            add_input(B - 1)

        @block.tensor
        def _(pe):
            def transposes(b, n):
                if not is_zero(b):
                    pe.wait_ge(s_tev, 6 * b - (4, 0)[n])
                for t in range(T):
                    if t % 2 == 0:
                        pe.wait_ge(s_xn, 4 * b + 2 * n + t // 2 + 1)
                    for f in range(FT):
                        last = nc.tensor.transpose(trn[FT * n + f][:, bass.ts(t, P)],
                                                   xn[:, n, t, bass.ts(f, P)], ident[:, :])
                        if t == T - 1:
                            last.then_inc(s_tr, 1)

            def projection_step(k, f):
                r = nc.tensor.matmul(prj[k], w_sb["qk"[k // 2]][:, f, bass.ts(k % 2, P)], lnT[:, k // 2, f, :],
                                     start=(f == 0), stop=(f == FT - 1))
                if f == FT - 1:
                    r.then_inc(s_prj, 1)

            def projections(b, n, halves=(0, 1)):
                pe.wait_ge(s_tev, 6 * b + 2 * n + 2)
                for k in (2 * n + half for half in halves):
                    if not is_zero(b):
                        if n == 0:
                            pe.wait_ge(s_vev, 2 * b - 1 + k)
                        else:
                            pe.wait_ge(s_rest, 4 * b)
                    for f in range(FT):
                        projection_step(k, f)

            def values_step(k, h, bank):
                for f in range(FT):
                    r = nc.tensor.matmul(bank[:, bass.ts(h, DM)], lnT[:, 2, f, bass.ts(2 * k + h, P)],
                                         w_sb["v"][:, f, :], start=(f == 0), stop=(f == FT - 1))
                if h:
                    r.then_inc(s_vprj, 1)

            def values(b, k):
                pe.wait_ge(s_tev, 6 * b + 6)
                pe.wait_ge(s_rest, 4 * b + k + 1)
                for h in range(2):
                    values_step(k, h, vps[k])

            def max_tile(b, n):
                g, t, j = n // TILES, n % TILES // G, n % G
                b, g = b + g // UNITS, g % UNITS
                if n % TILES == 0:
                    pe.wait_ge(s_load[g], 2 * DMA * (b + 1))
                if is_zero(b) and 0 < n < 2 * EARLY_PAIRS:
                    if j % 2 == 0:
                        pe.wait_ge(s_red, n // 2)
                elif j % 2 == 0 and n:
                    pe.wait_ge(s_red, (TILES * UNITS * b + n % (TILES * UNITS)) // 2 - 1 if isinstance(b, int)
                               else TILES * UNITS // 2 * b + n % (TILES * UNITS) // 2 - 1)
                bank = early_mx if is_zero(b) and n < 2 * EARLY_PAIRS else mx_ps[j // 2]
                r = nc.tensor.matmul(bank[:, j % 2, :], qs[0:ROWS, g, j, bass.ts(t, P)], ks[0:ROWS, g, j, :],
                                     start=True, stop=True)
                if j % 2:
                    r.then_inc(s_mx, 1)

            def max_transpose(b, slot, par):
                w = UNITS * b + slot
                pe.wait_ge(s_mp, w + 1)
                wait_alone(pe, "pe", s_mtev, w)
                nc.tensor.transpose(mt_ps[0:MROWS * G * T, :], m_parts[:, par].rearrange("p c n -> p (c n)"),
                                    ident_b[:, :]).then_inc(s_mt, 1)

            def score_tile(b, m, last=False):
                g, t, j = m // TILES, m % TILES // G, m % G
                if m % TILES == 0:
                    pe.wait_ge(s_mrow[g], DMA * (b + 1))
                bank, back = score_bank(m, last)
                if m > 1:
                    pe.wait_ge(s_exp, TILES * UNITS * b + m + 1 - back)
                elif m == 0:
                    pe.wait_ge(s_exp, TILES * UNITS * b)
                if last and m in (TAIL + 2, TAIL + 3):
                    pe.wait_ge(s_red, TILES * UNITS * B // 2)
                nc.tensor.matmul(bank, ks[0:ROWS + MROWS, g, j, bass.ts(t, P)], qs[0:ROWS + MROWS, g, j, :],
                                 start=True, stop=True).then_inc(s_st, 1)

            def values_product(b, q, half):
                g, t = q // T, q % T
                u = UNITS * b + g
                if half == 0:
                    if t == 0:
                        pe.wait_ge(s_vst, u + 1)
                        pe.wait_ge(s_oev, u)
                    pe.wait_ge(s_exp, TILES * UNITS * b + G * (q + 1))
                own = bass.ts(half, S // 2)
                for j in range(G):
                    last = nc.tensor.matmul(pv_ps[32 * j:32 * j + 32, own], v_st[:, g, t, j, :],
                                            probs[:, q % 4, j, own], start=(t == 0 and half == 0),
                                            stop=(t == T - 1 and half == 1), skip_group_check=True)
                if half:
                    last.then_inc(s_pv, 1)

            def output_tile(b, t):
                if b >= 2:
                    pe.wait_ge(s_fin, T * (b - 2) + t + 1)
                if (b, t) == (1, T - 1):
                    pe.wait_ge(s_oev, B * UNITS)
                pe.wait_ge(s_ct, (T + 1) * b + t + 2)
                for half in range(2):
                    last = nc.tensor.matmul(fc_ps[b % 2][t], ctxT[:, b % 2, half, bass.ts(t, P)],
                                            w_sb["fc"][:, half, :], start=(half == 0), stop=(half == 1))
                last.then_inc(s_fc, 1)

            def quad(b, q, last=False, first=False):
                score, bound = G * q, TILES * UNITS if last else 2 * TILES * UNITS
                for half in range(2):
                    for j in (2 * half, 2 * half + 1):
                        score_tile(b, score + j, last)
                        if score + j + LEAD < bound:
                            max_tile(b, score + j + LEAD)
                    if last and (q, half) in EARLY_OUT:
                        pe.wait_ge(s_red, TILES * UNITS * B // 2)
                        output_tile(*EARLY_OUT[q, half])
                    if q:
                        values_product(b, q - 1, half)
                    elif not first:
                        values_product(b - 1, QUADS - 1, half)
                    if half == 0 and q % T == T - 2 and not (last and q > QUADS - T):
                        max_transpose(b, q // T + 1, (q // T + 1) % 2)

            pe.wait_ge(s_heat, 1)
            for k in range(16):
                nc.tensor.matmul(ps[:, 7], heat[:, 0:P], heat[:, :], start=True, stop=True)
            pe.wait_ge(s_cst, 2 * DMA)
            transposes(0, 0)
            for k in range(4):
                nc.tensor.matmul(ps[:, 7], heat[:, 0:P], heat[:, :], start=True, stop=True)
            pe.wait_ge(s_wq, DMA)
            projections(0, 0, (0,))
            transposes(0, 1)
            projections(0, 0, (1,))
            pe.wait_ge(s_w, 4 * DMA)
            def phase1(i, early=False):
                projections(i, 1)
                values(i, 0)
                transposes(i + 1, 0)
                values(i, 1)
                if early:
                    pe.wait_ge(s_rest, 4 * i + 4)
                    max_tile(0, 0)
                    max_tile(0, 1)
                transposes(i + 1, 1)
                projections(i + 1, 0, (0,))
                if early:
                    max_tile(0, 2)
                    max_tile(0, 3)
                projections(i + 1, 0, (1,))

            with pe.Fori(0, B - 2) as i:
                phase1(i)
            phase1(B - 2, early=True)

            done = B - 1
            steps = [("k", k, f) for k in (2, 3) for f in range(FT)] + [("v", k, h) for k in range(2) for h in range(2)]
            pe.wait_ge(s_ones, 1)
            pe.wait_ge(s_tev, 6 * done + 6)
            pe.wait_ge(s_red, EARLY_PAIRS)
            for n in range(2 * EARLY_PAIRS, LEAD):
                if n == 2 * EARLY_PAIRS + 2:
                    pe.wait_ge(s_rest, 4 * done + 2)
                if n == TILES + 4:
                    pe.wait_ge(s_ib, 1)
                    pe.wait_ge(s_rest, 4 * B)
                    max_transpose(0, 0, 0)
                max_tile(0, n)
                if n % 2 and (n < TILES or n in (TILES + 3, TILES + 5)):
                    kind, k, part = steps.pop(0)
                    if kind == "k":
                        projection_step(k, part)
                    else:
                        if (k, part) == (1, 0):
                            pe.wait_ge(s_rest, 4 * done + 3)
                        values_step(k, part, vps_last[k])
            pe.wait_ge(s_vev, 2 * B - 1)
            quad(0, 0, first=True)
            pe.wait_ge(s_vev, 2 * B)
            pe.wait_ge(s_vones, 1)
            with pe.Fori(0, B - 1) as b:
                for q in range(1, QUADS):
                    quad(b, q)
                quad(b + 1, 0)
            for q in range(1, QUADS):
                quad(B - 1, q, last=True)
            pe.wait_ge(s_mtev, B * UNITS)
            output_tile(*EARLY_OUT[QUADS, 0])
            for half in range(2):
                values_product(B - 1, QUADS - 1, half)

            for b in range(B):
                for t in range(T):
                    if (b, t) not in EARLY_OUT.values():
                        output_tile(b, t)


def kernel(x, ctx_1024, L0_xattn_ln_q_g, L0_xattn_ln_q_b, L0_xattn_ln_k_g, L0_xattn_ln_k_b, L0_xattn_ln_v_g,
           L0_xattn_ln_v_b, L0_xattn_w_q, L0_xattn_w_k, L0_xattn_w_v, L0_xattn_w_fc, L0_xattn_b_fc):
    import numpy as np
    import concourse.bacc as bacc
    from concourse.bass_utils import run_bass_kernel_spmd

    def by_dimension(w):
        return np.ascontiguousarray(np.asarray(w).T.reshape(DM, 2, HEADS // 2, HD).transpose(0, 1, 3, 2)
                                    .reshape(DM, DM))

    vectors = (L0_xattn_ln_q_g, L0_xattn_ln_q_b, L0_xattn_ln_k_g, L0_xattn_ln_k_b, L0_xattn_ln_v_g, L0_xattn_ln_v_b)
    arrays = {
        "x": np.asarray(x),
        "context": np.asarray(ctx_1024),
        "wqT": by_dimension(L0_xattn_w_q),
        "wkT": by_dimension(L0_xattn_w_k),
        "wvT": np.ascontiguousarray(np.asarray(L0_xattn_w_v).T),
        "wfcT": np.ascontiguousarray(np.asarray(L0_xattn_w_fc).T.reshape(2, UNITS // 2, G, HD, DM)
                                     .transpose(0, 1, 3, 2, 4).reshape(DM, DM)),
        "ln_cols": np.ascontiguousarray(np.stack([np.asarray(v).reshape(FT, P) for v in vectors]).transpose(2, 0, 1)),
        "b_fc": np.asarray(L0_xattn_b_fc),
        "eye": np.eye(P, dtype=np.float32),
    }
    nc = bacc.Bacc("TRN2", target_bir_lowering=False, num_devices=1)
    args = [nc.dram_tensor(n, a.shape, mybir.dt.from_np(a.dtype), kind="ExternalInput").ap()
            for n, a in arrays.items()]
    out = nc.dram_tensor("out", (B, S, DM), F32, kind="ExternalOutput").ap()
    build(nc, *args, out)
    result = run_bass_kernel_spmd(nc, [arrays], core_ids=[0])
    return result.results[0]["out"]
```
